# Optimizing a Trainium2 kernel written in Bass

```python
import numpy as np
import jax
import jax.numpy as jnp

def _softmax(x, axis=-1):
    return jax.nn.softmax(x, axis=axis)

def _gelu(x):
    return jax.nn.gelu(x, approximate=True)

def _silu(x):
    return jax.nn.silu(x)

def _sigmoid(x):
    return jax.nn.sigmoid(x)

def _layernorm(x, axis=-1, eps=1e-05):
    m = jnp.mean(x, axis=axis, keepdims=True)
    v = jnp.var(x, axis=axis, keepdims=True)
    return (x - m) / jnp.sqrt(v + eps)

def _scatter_add(tgt, idx, src, axis=0):
    return tgt.at[idx].add(src)

def _segment_sum(src, seg, n):
    return jax.ops.segment_sum(src, seg, n)
kernel_name = 'mk_xattn_ffn_d1_seqx_r2_ae0200'

def setup_inputs(seed: int=0):
    np.random.seed(seed)
    _w = jnp.asarray

    def _rec_inputs():
        import jax
        import jax.numpy as jnp
        _rk = jax.random.key(seed)
        x = 7.22e-05 + 1 * jax.random.normal(jax.random.fold_in(_rk, 1), (8, 1024, 1024), jnp.float32)
        _lenS = 1024 - jax.random.randint(jax.random.fold_in(_rk, 7), (8,), 0, max(1, 1024 // 4) + 1, jnp.int32)
        _lenS2 = 64 - jax.random.randint(jax.random.fold_in(_rk, 8), (8,), 0, max(1, 64 // 4) + 1, jnp.int32)
        _ctx_512P = jax.random.normal(jax.random.fold_in(_rk, 11), (8, 16, 256), jnp.float32)
        _ctx_512c = jax.random.dirichlet(jax.random.fold_in(_rk, 511), 0.3 * jnp.ones((16,), jnp.float32), (8, 64))
        _ctx_512t = jnp.einsum('bsk,bkd->bsd', _ctx_512c, _ctx_512P)
        _ctx_512t = _ctx_512t * jax.lax.rsqrt(jnp.mean(jnp.square(_ctx_512t)) + 1e-12) * 0.953939
        ctx_512 = -0.000514642 + 1.00011 * (_ctx_512t + 0.3 * jax.random.normal(jax.random.fold_in(_rk, 611), (8, 64, 256), jnp.float32))
        return (x, ctx_512)
    x, ctx_512 = _rec_inputs()

    def _L0_xattn_setup():
        import jax, jax.numpy as jnp
        import numpy as np
        B, S, H, NH, L = (2, 1024, 1024, 16, 256)
        HD = H // NH
        key = jax.random.key(seed)
        k1, k2, k3, k4, k5 = jax.random.split(key, 5)
        scale = 0.02
        return {'q': jax.random.normal(k1, (B, S, H), dtype=jnp.float32), 'latent_kv': jax.random.normal(k2, (B, S, L), dtype=jnp.float32), 'Wq': jax.random.normal(k3, (H, H), dtype=jnp.float32) * scale, 'Wkv_expand': jax.random.normal(k4, (2 * H, L), dtype=jnp.float32) * scale, 'Wout': jax.random.normal(k5, (H, H), dtype=jnp.float32) * scale}
    _L0_xattn_all = _L0_xattn_setup()
    _L0_xattn_in = {k: v for k, v in _L0_xattn_all.items() if k in ('Wq', 'Wkv_expand', 'Wout')}
    del _L0_xattn_all

    def _L0_ffn_setup():
        import jax, jax.numpy as jnp
        import numpy as np
        E4M3_MAX = 448.0

        def _quant_e4m3(t):
            amax = jnp.max(jnp.abs(t)).astype(jnp.float32)
            scale = jnp.maximum(amax / E4M3_MAX, 1e-12)
            fp8 = (t.astype(jnp.float32) / scale).astype(jnp.float8_e4m3fn)
            return (fp8, scale)

        def _scaled_mm(a_fp8, b_fp8, sa, sb):
            acc = jnp.matmul(a_fp8.astype(jnp.float32), b_fp8.astype(jnp.float32))
            return (acc * (sa * sb)).astype(jnp.bfloat16)
        key = jax.random.key(seed)
        k1, k2 = jax.random.split(key)
        x = jax.random.normal(k1, (4, 1024, 1024), dtype=jnp.bfloat16)
        weight = (jax.random.normal(k2, (1024, 1024), dtype=jnp.bfloat16) * 0.02).astype(jnp.bfloat16)
        return {'x': x, 'weight': weight}
    _L0_ffn_all = _L0_ffn_setup()
    _L0_ffn_in = {k: v for k, v in _L0_ffn_all.items() if k in ('weight',)}
    del _L0_ffn_all
    return {'x': x, 'ctx_512': ctx_512, 'L0_xattn_Wq': _L0_xattn_in['Wq'], 'L0_xattn_Wkv_expand': _L0_xattn_in['Wkv_expand'], 'L0_xattn_Wout': _L0_xattn_in['Wout'], 'L0_ffn_weight': _L0_ffn_in['weight']}

def reference(x, ctx_512, L0_xattn_Wq, L0_xattn_Wkv_expand, L0_xattn_Wout, L0_ffn_weight):
    import jax
    import jax.numpy as jnp

    def _L0_xattn_ref(q, latent_kv, Wq, Wkv_expand, Wout):
        import jax, jax.numpy as jnp
        import numpy as np
        B, S, H, NH, L = (2, 1024, 1024, 16, 256)
        HD = H // NH
        b, sq, _ = q.shape
        sk = latent_kv.shape[1]
        qp = q @ Wq.T
        kv = latent_kv @ Wkv_expand.T
        k, v = jnp.split(kv, 2, axis=-1)
        qh = qp.reshape(b, sq, NH, HD).transpose(0, 2, 1, 3)
        kh = k.reshape(b, sk, NH, HD).transpose(0, 2, 1, 3)
        vh = v.reshape(b, sk, NH, HD).transpose(0, 2, 1, 3)
        inv_sqrt_d = 1.0 / jnp.sqrt(jnp.float32(HD))
        scores = jnp.einsum('bhqd,bhkd->bhqk', qh, kh) * inv_sqrt_d
        causal = jnp.tril(jnp.ones((sq, sk), dtype=bool))
        scores = jnp.where(causal, scores, jnp.finfo(scores.dtype).min)
        attn = jax.nn.softmax(scores, axis=-1)
        out = jnp.einsum('bhqk,bhkd->bhqd', attn, vh)
        out = out.transpose(0, 2, 1, 3).reshape(b, sq, H)
        return out @ Wout.T

    def _L0_ffn_ref(x, weight):
        import jax, jax.numpy as jnp
        import numpy as np
        E4M3_MAX = 448.0

        def _quant_e4m3(t):
            amax = jnp.max(jnp.abs(t)).astype(jnp.float32)
            scale = jnp.maximum(amax / E4M3_MAX, 1e-12)
            fp8 = (t.astype(jnp.float32) / scale).astype(jnp.float8_e4m3fn)
            return (fp8, scale)

        def _scaled_mm(a_fp8, b_fp8, sa, sb):
            acc = jnp.matmul(a_fp8.astype(jnp.float32), b_fp8.astype(jnp.float32))
            return (acc * (sa * sb)).astype(jnp.bfloat16)
        w_fp8, w_scale = _quant_e4m3(weight)
        x2d = x.reshape(-1, x.shape[-1])
        x_fp8, x_scale = _quant_e4m3(x2d)
        out2d = _scaled_mm(x_fp8, w_fp8.T, x_scale, w_scale)
        return out2d.reshape(*x.shape[:-1], out2d.shape[-1])
    x = x + _L0_xattn_ref(_layernorm(x, axis=-1), ctx_512, L0_xattn_Wq, L0_xattn_Wkv_expand, L0_xattn_Wout)
    x = x + _L0_ffn_ref(_layernorm(x, axis=-1), L0_ffn_weight)
    return x

_drawn_inputs = setup_inputs


def setup_inputs(seed=0):
    import zlib

    import numpy as np

    out = dict(_drawn_inputs(seed))
    spreads = {}
    factors = {'L0_xattn_Wq': 4.578}
    for name, (base, spread) in spreads.items():
        noise = np.random.default_rng([zlib.crc32(name.encode()), seed]).standard_normal(out[name].shape)
        drawn = base * np.exp(spread * noise) if base else spread * noise
        out[name] = jnp.asarray(drawn.astype(out[name].dtype))
    for name, factor in factors.items():
        out[name] = (out[name] * factor).astype(out[name].dtype)
    return out
```

```python
from contextlib import ExitStack

import concourse.bass as bass
from concourse import mybir

F32 = mybir.dt.float32
F16 = mybir.dt.float16
BF16 = mybir.dt.bfloat16
U32 = mybir.dt.uint32
ALU = mybir.AluOpType
ACT = mybir.ActivationFunctionType
AX = mybir.AxisListType
ROWS_MAX = bass.bass_isa.ReduceOp.max

P = 128
HD = 64
LN_EPS = 1e-5
E4M3_MAX = 448.0

AMAX_TO = 2.0 ** 13
MN_SCALE = 2.0 ** -20
XN_SCALE = 2.0 ** 10
P_SCALE = 2.0 ** 14
AMAX_FLOOR = 2.0 ** -40
ROUND_SHIFT = 2.0 ** 20
ROUND_LEAST = 1.5 * 2.0 ** 14
EXPONENT_BITS = 0x7F800000
HALF_BIT = 0x00400000
MASKED = -3.0e38


def xattn_ffn_kernel(nc, x, ctx, Wq, Wkv, Wout, Wffn, out):
    B, S, H = x.shape
    SK, L = ctx.shape[1:]
    NH = H // HD
    NP = NH // 2
    CT = H // P
    LT = L // P
    TB = S // P
    T = B * TB
    KEYS = B * SK
    HALF = 512
    assert SK == HD and NP == CT and KEYS == HALF and TB == 8

    x_rows = x.rearrange("b s h -> (b s) h")
    out_rows = out.rearrange("b s h -> (b s) h")

    with ExitStack() as scope:
        def sb(name, shape, dt):
            return scope.enter_context(nc.sbuf_tensor(name, shape, dt))

        def sem(name):
            return scope.enter_context(nc.semaphore(name))

        x1_dram = nc.dram_tensor("x1_scratch", [T * P, H], F32, kind="Internal").ap()
        k_dram = nc.dram_tensor("k_scratch", [B, 2, HD, NH, SK], F16, kind="Internal").ap()
        v_dram = nc.dram_tensor("v_scratch", [B, 2, 2, HD, NP, SK], F16, kind="Internal").ap()

        wq_stack = sb("wq_stack", [P, NH, H], F16)
        wo_t = sb("wo_t", [P, 2, NP, H], F16)
        m_buf = sb("m_buf", [P, 2, CT, H], F16)
        n_buf = sb("n_buf", [P, 2, NP, H], F16)
        k_hilo = sb("k_hilo", [P, NH, SK], F16)
        k_lohi = sb("k_lohi", [P, NH, SK], F16)
        v_diag = sb("v_diag", [P, 2, NP, P], F16)

        tile_space = sb("tile_space", [P, 14, H], F32)
        xt_buf = tile_space[:, 11, :].bitcast(F16).rearrange("p (s n) -> p s n", s=2)
        pt_buf = tile_space[:, 12, :].bitcast(F16).rearrange("p (s n) -> p s n", s=2)
        xa = [tile_space[:, i, :] for i in (0, 1)]
        xr = [tile_space[:, i, :] for i in (2, 3)]
        xn = [tile_space[:, i, :] for i in (4, 5)]
        x1 = [tile_space[:, i, :] for i in (6, 7)]
        sub = tile_space[:, 8, :]
        ex = tile_space[:, 9, :]
        pr = tile_space[:, 10, :]
        dev = tile_space[:, 13, :]

        ident = sb("ident", [P, P], F32)
        ident_bf = sb("ident_bf", [P, P], BF16)
        causal = sb("causal", [P, SK], F32)
        minus_half = sb("minus_half", [P, T], F32)
        amax4 = sb("amax4", [P, 4], F32)
        amax4_all = sb("amax4_all", [P, 4], F32)
        to_f16 = sb("to_f16", [P, 4], F32)
        from_f16 = sb("from_f16", [P, 4], F32)
        score_scale = sb("score_scale", [P, 1], F32)
        out_scale = sb("out_scale", [P, 1], F32)
        small = sb("small", [P, 16], F32)
        stats_a = sb("stats_a", [P, 2, 6], F32)
        stats_b = sb("stats_b", [P, 2, 6], F32)
        mv_a = [sb(f"mv_a{i}", [P, 2], F32) for i in (0, 1)]
        mv_b = sb("mv_b", [P, 2], F32)
        veps = [sb(f"veps_x{i}", [P, 1], F32) for i in (0, 1)]
        rstd = [sb(f"rstd_x{i}", [P, 1], F32) for i in (0, 1)]
        neg_mean = [sb(f"neg_mean{i}", [P, 1], F32) for i in (0, 1)]
        wait_carrier = sb("wait_carrier", [P, 1], F32)
        hmax = sb("hmax", [P, NH], F32)
        hsum = sb("hsum", [P, NH], F32)
        hinv = sb("hinv", [P, NH], F32)
        mean1 = sb("mean1", [P, T], F32)
        var1 = sb("var1", [P, T], F32)
        rstd1 = sb("rstd1", [P, T], F32)
        peak1 = sb("peak1", [P, T], F32)
        quant_a = sb("quant_a", [P, T], F32)
        quant_b = sb("quant_b", [P, T], F32)
        quant_a20 = sb("quant_a20", [P, T], F32)
        quant_b20 = sb("quant_b20", [P, T], F32)

        ps_s = scope.enter_context(nc.psum_tensor("ps_s", [P, H], F32))
        ps_o = scope.enter_context(nc.psum_tensor("ps_o", [P, H], F32))
        ps_x = scope.enter_context(nc.psum_tensor("ps_x", [P, H], F32))
        ps_p = scope.enter_context(nc.psum_tensor("ps_p", [P, H], F32))

        wq_f = [m_buf[:].rearrange("p a b c -> p (a b c)").bitcast(F32).rearrange("p (h c) -> p h c", c=H),
                n_buf[:].rearrange("p a b c -> p (a b c)").bitcast(F32).rearrange("p (h c) -> p h c", c=H)]
        wout_f = tile_space[:, 0:8, :]
        wkv_f = tile_space[:, 8:12, :].rearrange("p a (b l) -> p (a b) l", l=L)
        ctx_f = tile_space[:, 12, :].rearrange("p (a l) -> p a l", l=L)
        front = wq_stack[:].rearrange("p h c -> p (h c)")
        wkv_t = front[:, 0:8192].bitcast(F32).rearrange("p (a r) -> p a r", a=LT)
        ctx_t = front[:, 8192:10240].bitcast(F32).rearrange("p (a k) -> p a k", a=LT)
        kv_f = wo_t[:].rearrange("p a b c -> p (a b c)").bitcast(F32).rearrange("p (g k) -> p g k", k=KEYS)
        kv_hi = tile_space[:, 8:12, :].rearrange("p a c -> p (a c)").bitcast(F16).rearrange("p (g k) -> p g k", k=KEYS)
        kv_lo = front[:, 0:8192].rearrange("p (g k) -> p g k", k=KEYS)
        NG = 2 * NP

        const_made = sem("const_made")
        diag_zeroed = sem("diag_zeroed")
        got_ctx = sem("got_ctx")
        got_wkv = [sem(f"got_wkv{q}") for q in range(4)]
        got_wout = sem("got_wout")
        got_wq = [sem("got_wq0"), sem("got_wq1")]
        turned = sem("turned")
        turned_read = sem("turned_read")
        amax_rows = sem("amax_rows")
        amax_done = sem("amax_done")
        scales_made = sem("scales_made")
        dve_step = sem("dve_step")
        act_hi0 = sem("act_hi0")
        kv_split = sem("kv_split")
        kv_stored = sem("kv_stored")
        wq_ready = sem("wq_ready")
        got_k = sem("got_k")
        got_v = sem("got_v")
        got_xa = [sem("got_xa0"), sem("got_xa1")]
        got_xr = [sem("got_xr0"), sem("got_xr1")]
        var_ready = sem("var_ready")
        rstd_ready = sem("rstd_ready")
        xn_ready = sem("xn_ready")
        x_full = sem("x_full")
        x_hi = sem("x_hi")
        x_free = sem("x_free")
        p_full = sem("p_full")
        p_hi = sem("p_hi")
        p_free = sem("p_free")
        s_full = sem("s_full")
        s_read = sem("s_read")
        exp_done = sem("exp_done")
        p_ready = sem("p_ready")
        o_full = sem("o_full")
        x1_ready = sem("x1_ready")
        a_stats = sem("a_stats")
        a_aggr = sem("a_aggr")
        b_stats = sem("b_stats")
        b_aggr = sem("b_aggr")
        masked = sem("masked")
        max_done = sem("max_done")
        sum_done = sem("sum_done")
        inv_done = sem("inv_done")
        kept = sem("kept")
        mean_ready = sem("mean_ready")
        dev_ready = sem("dev_ready")
        x1_done = sem("x1_done")
        x1_stored = [sem("x1_stored0"), sem("x1_stored1")]
        var1_ready = sem("var1_ready")
        rstd1_ready = sem("rstd1_ready")
        got_w8 = sem("got_w8")
        w_amax_rows = sem("w_amax_rows")
        w_amax_done = sem("w_amax_done")
        x_amax_rows = sem("x_amax_rows")
        x_amax_done = sem("x_amax_done")
        w8_ready = sem("w8_ready")
        w8_full = sem("w8_full")
        w8_read = sem("w8_read")
        quant_ready = sem("quant_ready")
        chain2 = sem("chain2")
        g_done = sem("g_done")
        a_done = sem("a_done")
        got_x1 = [sem(f"got_x1_{i}") for i in range(8)]
        v_ready = sem("v_ready")
        r_ready = sem("r_ready")
        r_full = sem("r_full")
        rt_ready = sem("rt_ready")
        y_full = sem("y_full")
        y_ready = sem("y_ready")
        sum_ready = sem("sum_ready")
        out_stored = [sem(f"out_stored{i}") for i in range(8)]

        flat_m = m_buf[:].rearrange("p a b c -> p (a b c)")
        flat_n = n_buf[:].rearrange("p a b c -> p (a b c)")
        w8_raw = wo_t[:].rearrange("p a b c -> p (a b c)")[:, 0:8192].bitcast(BF16).rearrange("p (a c) -> p a c", c=H)
        w8_q = wo_t[:].rearrange("p a b c -> p (a b c)")[:, 8192:16384].bitcast(BF16).rearrange("p (a c) -> p a c", c=H)
        w8_t = flat_m[:, 0:8192].bitcast(BF16).rearrange("p (a c) -> p a c", c=H)
        w_tmp = [flat_n[:, i * 2048:(i + 1) * 2048].bitcast(F32) for i in range(4)]
        X2 = 8
        x2 = [tile_space[:, i, :] for i in range(X2)]
        v_t = [flat_n[:, i * 2048:(i + 1) * 2048].bitcast(F32) for i in (4, 5)]
        u_t = [flat_n[:, i * 2048:(i + 1) * 2048].bitcast(F32) for i in (6, 7)]
        g_t = tile_space[:, 8, :]
        a_t = tile_space[:, 9, :]
        r_t = [tile_space[:, 10, :].bitcast(BF16)[:, i * H:(i + 1) * H] for i in (0, 1)]
        rt_t = [tile_space[:, 11, :].bitcast(BF16)[:, i * H:(i + 1) * H] for i in (0, 1)]
        y_t = [tile_space[:, 12, :].bitcast(BF16)[:, i * H:(i + 1) * H] for i in (0, 1)]
        r_ps = [ps_x[:, 0:512].bitcast(BF16), ps_p[:, 0:512].bitcast(BF16)]
        y_ps = [ps_s, ps_o]
        w8_ps = [ps_x[:, 512:1024].bitcast(BF16), ps_p[:, 512:1024].bitcast(BF16)]

        slots0 = [ps_s, ps_o, ps_x, ps_p]
        USES_CTX, USES_WKV, USES_KV, USES_WOUT = 1, 4, NG // 2, CT
        USES0 = USES_CTX + USES_WKV + USES_KV + USES_WOUT

        def x_uses(b, tt):
            return b * (TB + CT) + tt + CT + 2

        def p_uses(b, tt):
            return b * (TB + CT) + tt + CT

        block = scope.enter_context(nc.Block())

        @block.sync
        def _(sp):
            ctx_rows = ctx.rearrange("b k l -> (b k) l").rearrange("(a p) l -> p a l", p=P)
            sp.dma_start(ctx_f, ctx_rows).then_inc(got_ctx, 16)
            wkv_rows = Wkv.rearrange("(a p) l -> p a l", p=P)
            for q in range(4):
                sp.dma_start(wkv_f[:, 4 * q:4 * q + 4, :], wkv_rows[:, 4 * q:4 * q + 4, :]).then_inc(got_wkv[q], 16)
            wq_rows = Wq.rearrange("(h d) c -> d h c", d=HD)
            for half in range(2):
                for dup in range(2):
                    sp.dma_start(wq_f[half][dup * HD:(dup + 1) * HD], wq_rows[:, half * NP:(half + 1) * NP, :]).then_inc(got_wq[half], 16)
            wout_rows = Wout.rearrange("(a p) c -> p a c", p=P)
            for q in range(2):
                sp.dma_start(wout_f[:, 4 * q:4 * q + 4, :], wout_rows[:, 4 * q:4 * q + 4, :]).then_inc(got_wout, 16)

            sp.wait_ge(kv_split, 1)
            for b in range(B):
                for part, src in ((0, kv_hi), (1, kv_lo)):
                    for e in range(2):
                        rows = slice(e * HD, (e + 1) * HD)
                        keys = slice(b * SK, (b + 1) * SK)
                        k_to = k_dram[b, part].rearrange("d (j e) k -> e d j k", e=2)[e]
                        sp.dma_start(k_to, src[rows, 0:NP, keys]).then_inc(kv_stored, 16)
                        sp.dma_start(v_dram[b, part, e], src[rows, NP:NG, keys]).then_inc(kv_stored, 16)
            sp.wait_ge(kv_stored, 16 * 8 * B)

            def load_k(b):
                sp.dma_start(k_hilo[:], k_dram[b].rearrange("s d h k -> (s d) h k")).then_inc(got_k, 16)
                for part in range(2):
                    sp.dma_start(k_lohi[part * HD:(part + 1) * HD], k_dram[b, 1 - part]).then_inc(got_k, 16)

            def load_v(b):
                for part in range(2):
                    for e in range(2):
                        rows = slice(e * HD, (e + 1) * HD)
                        sp.dma_start(v_diag[rows, part, :, rows], v_dram[b, part, e]).then_inc(got_v, 16)

            def load_x(to, got, t, e):
                sp.dma_start(to[e], x_rows[bass.ds(t * P, P), :]).then_inc(got[e], 16)

            load_k(0)
            sp.wait_ge(diag_zeroed, 1)
            load_v(0)
            sp.wait_ge(turned, USES0)
            for t in range(2):
                load_x(xa, got_xa, t, t)
            load_x(xr, got_xr, 0, 0)
            for t in range(2, 4):
                sp.wait_ge(xn_ready, t - 1)
                load_x(xa, got_xa, t, t % 2)

            def step(t, e, norm=True, residual=True, store=True):
                if norm:
                    sp.wait_ge(xn_ready, t + 3)
                    load_x(xa, got_xa, t + 4, e)
                if store:
                    sp.wait_ge(x1_ready, t)
                if residual:
                    load_x(xr, got_xr, t + 1, 1 - e)
                if store:
                    sp.dma_start(x1_dram[bass.ds((t - 1) * P, P), :], x1[1 - e]).then_inc(x1_stored[1 - e], 16)

            def next_kv(b):
                sp.wait_ge(p_full, p_uses(b - 1, 0) - CT // 2)
                load_k(b)
                sp.wait_ge(p_full, p_uses(b - 1, 0))
                load_v(b)

            step(0, 0, store=False)
            step(1, 1)
            next_kv(1)
            with sp.Fori(0, TB // 2 - 1) as j:
                step(2 * j + 2, 0)
                step(2 * j + 3, 1)
            with sp.Fori(1, B - 1) as b:
                step(b * TB, 0)
                step(b * TB + 1, 1)
                next_kv(b + 1)
                with sp.Fori(0, TB // 2 - 1) as j:
                    step(b * TB + 2 * j + 2, 0)
                    step(b * TB + 2 * j + 3, 1)
            sp.wait_ge(p_full, p_uses(B - 1, 0))
            w_rows = Wffn.rearrange("(a p) c -> p a c", p=P)
            sp.dma_start(w8_raw, w_rows).then_inc(got_w8, 16)
            for t in range(T - TB, T):
                step(t, t % 2, norm=t + 4 < T, residual=t + 1 < T)
            sp.wait_ge(x1_ready, T)
            sp.dma_start(x1_dram[(T - 1) * P:T * P, :], x1[(T - 1) % 2]).then_inc(x1_stored[(T - 1) % 2], 16)

            for e in range(2):
                sp.wait_ge(x1_stored[e], 16 * (T // 2))
            sp.wait_ge(x1_done, T)
            sp.wait_ge(rstd1_ready, 1)

            def load_x1(t, i):
                sp.dma_start(x2[i], x1_dram[bass.ds(t * P, P), :]).then_inc(got_x1[i], 16)

            for t in range(X2):
                load_x1(t, t)

            def store_out(t, i):
                sp.wait_ge(sum_ready, t + 1)
                sp.dma_start(out_rows[bass.ds(t * P, P), :], x2[i]).then_inc(out_stored[i], 16)

            with sp.Fori(0, T // X2 - 1) as q:
                for i in range(X2):
                    store_out(q * X2 + i, i)
                    if i % 2:
                        for k in (i - 1, i):
                            sp.wait_ge(out_stored[k], q * 16 + 16)
                            load_x1((q + 1) * X2 + k, k)
            for i in range(X2):
                store_out(T - X2 + i, i)
            for i in range(X2):
                sp.wait_ge(out_stored[i], 16 * (T // X2))

        @block.gpsimd
        def _(pool):
            nc.gpsimd.memset(ident[:], 0.0).then_inc(const_made, 1)
            nc.gpsimd.memset(causal[:], 0.0).then_inc(const_made, 1)
            nc.gpsimd.memset(minus_half[:], -0.5).then_inc(const_made, 1)
            nc.gpsimd.memset(v_diag[:].rearrange("p a b c -> p (a b c)"), 0.0).then_inc(diag_zeroed, 1)
            pool.wait_ge(const_made, 3)
            nc.gpsimd.affine_select(out=ident[:], in_=ident[:], compare_op=ALU.not_equal, fill=1.0, base=0,
                                    pattern=[[-1, P]], channel_multiplier=1).then_inc(const_made, 1)
            nc.gpsimd.affine_select(out=causal[:], in_=causal[:], compare_op=ALU.is_ge, fill=MASKED, base=0,
                                    pattern=[[-1, SK]], channel_multiplier=1).then_inc(const_made, 1)
            pool.wait_ge(const_made, 5)
            nc.gpsimd.tensor_copy(ident_bf[:], ident[:]).then_inc(const_made, 1)
            pool.wait_ge(amax_rows, 1)
            nc.gpsimd.partition_all_reduce(amax4_all[:], amax4[:], P, ROWS_MAX).then_inc(amax_done, 1)

            def inverse_deviation(t, e):
                pool.wait_ge(var_ready, t + 1)
                nc.gpsimd.tensor_tensor(rstd[e][:], veps[e][:], minus_half[:, 0:1], ALU.pow).then_inc(rstd_ready, 1)

            with pool.Fori(0, T // 2) as j:
                inverse_deviation(2 * j, 0)
                inverse_deviation(2 * j + 1, 1)
            pool.wait_ge(w_amax_rows, 1)
            nc.gpsimd.partition_all_reduce(small[:, 1:2], small[:, 0:1], P, ROWS_MAX).then_inc(w_amax_done, 1)
            pool.wait_ge(var1_ready, 1)
            nc.gpsimd.tensor_tensor(rstd1[:], var1[:], minus_half[:], ALU.pow).then_inc(rstd1_ready, 1)
            pool.wait_ge(x_amax_rows, 1)
            nc.gpsimd.partition_all_reduce(small[:, 3:4], small[:, 2:3], P, ROWS_MAX).then_inc(x_amax_done, 1)

            with pool.Fori(0, T // X2) as q:
                for i in range(X2):
                    pool.wait_ge(y_ready, q * X2 + i + 1)
                    nc.gpsimd.tensor_tensor(x2[i], x2[i], y_t[i % 2], ALU.add).then_inc(sum_ready, 1)

        @block.tensor
        def _(pe):
            use = [0]

            def next_slot():
                n = use[0]
                use[0] += 1
                if n >= 4:
                    pe.wait_ge(turned_read, n - 3)
                return slots0[n % 4]

            pe.wait_ge(const_made, 6)
            pe.wait_ge(got_ctx, 16)
            to = next_slot()
            for lt in range(LT):
                for a in range(KEYS // P):
                    mm = nc.tensor.transpose(to[:, (lt * 4 + a) * P:(lt * 4 + a + 1) * P],
                                             ctx_f[:, a, lt * P:(lt + 1) * P], ident[:])
            mm.then_inc(turned, 1)
            for q in range(4):
                pe.wait_ge(got_wkv[q], 16)
                to = next_slot()
                for lt in range(LT):
                    for a in range(4):
                        mm = nc.tensor.transpose(to[:, (lt * 4 + a) * P:(lt * 4 + a + 1) * P],
                                                 wkv_f[:, 4 * q + a, lt * P:(lt + 1) * P], ident[:])
                mm.then_inc(turned, 1)
            for g2 in range(NG // 2):
                to = next_slot()
                if g2 == 0:
                    pe.wait_ge(turned_read, USES_CTX + USES_WKV)
                for half in range(2):
                    g = 2 * g2 + half
                    for lt in range(LT):
                        mm = nc.tensor.matmul(to[:, half * HALF:(half + 1) * HALF],
                                              wkv_t[:, lt, g * P:(g + 1) * P], ctx_t[:, lt, :],
                                              start=(lt == 0), stop=(lt == LT - 1))
                mm.then_inc(turned, 1)
            for j in range(NP):
                if j == 0:
                    pe.wait_ge(got_wout, 32)
                to = next_slot()
                for a in range(CT):
                    mm = nc.tensor.transpose(to[:, a * P:(a + 1) * P], wout_f[:, a, j * P:(j + 1) * P], ident[:])
                mm.then_inc(turned, 1)

            def make_m(b, x_before, p_before):
                pe.wait_ge(got_k, (b + 1) * 48)
                for ct in range(CT):
                    to, free, full, before = ((ps_x, x_free, x_full, x_before), (ps_p, p_free, p_full, p_before))[ct % 2]
                    n = before + ct // 2
                    if not (isinstance(n, int) and n == 0):
                        pe.wait_ge(free, n)
                    for h in range(NH):
                        cols = to[:, h * SK:(h + 1) * SK]
                        w = wq_stack[:, h, ct * P:(ct + 1) * P]
                        nc.tensor.matmul(cols, w, k_hilo[:, h, :], start=True, stop=False)
                        mm = nc.tensor.matmul(cols, w, k_lohi[:, h, :], start=False, stop=True)
                    mm.then_inc(full, 1)

            def make_n(b, x_before, p_before):
                pe.wait_ge(got_v, (b + 1) * 64)
                for j in range(NP):
                    to, free, full, before = ((ps_x, x_free, x_full, x_before), (ps_p, p_free, p_full, p_before))[j % 2]
                    pe.wait_ge(free, before + j // 2)
                    passes = ((0, 0), (0, 1), (1, 0))
                    for i, (vs, ws) in enumerate(passes):
                        for half in range(2):
                            cols = slice(half * HALF, (half + 1) * HALF)
                            mm = nc.tensor.matmul(to[:, cols], v_diag[:, vs, j, :], wo_t[:, ws, j, cols],
                                                  start=(i == 0), stop=(i == len(passes) - 1))
                    mm.then_inc(full, 1)

            def split_product(to, left, right, full):
                passes = ((0, 0), (0, 1), (1, 0))
                for c in range(CT):
                    for i, (ls, rs) in enumerate(passes):
                        for half in range(2):
                            cols = slice(half * HALF, (half + 1) * HALF)
                            mm = nc.tensor.matmul(to[:, cols], left[:, ls, c * P:(c + 1) * P], right[:, rs, c, cols],
                                                  start=(c == 0 and i == 0),
                                                  stop=(c == CT - 1 and i == len(passes) - 1))
                mm.then_inc(full, 1)

            def turn(to, tile, full):
                for c in range(CT):
                    mm = nc.tensor.transpose(to[:, c * P:(c + 1) * P], tile[:, c * P:(c + 1) * P], ident[:])
                mm.then_inc(full, 1)

            def step(b, tt, e, t, scores=True, x_next=True, first_m=False):
                xb, pb = x_uses(b, tt), p_uses(b, tt)
                pe.wait_ge(p_ready, t + 1)
                pe.wait_ge(p_free, pb)
                turn(ps_p, pr, p_full)
                grown = 0
                if first_m:
                    make_m(b + 1, xb, pb + 1)
                    grown = CT // 2
                if scores:
                    pe.wait_ge(x_free, xb + grown)
                    if first_m:
                        pe.wait_ge(p_free, pb + 1 + grown)
                    pe.wait_ge(s_read, t + 1)
                    split_product(ps_s, xt_buf, m_buf, s_full)
                if x_next:
                    pe.wait_ge(xn_ready, t + 3)
                    turn(ps_x, xn[e], x_full)
                pe.wait_ge(p_free, pb + 1)
                if not (isinstance(t, int) and t == 0):
                    pe.wait_ge(x1_ready, t)
                split_product(ps_o, pt_buf, n_buf, o_full)
                if first_m:
                    make_n(b + 1, xb + grown + 1, pb + 1 + grown)

            pe.wait_ge(turned_read, USES0)
            pe.wait_ge(wq_ready, 1)
            make_m(0, 0, 0)
            make_n(0, CT // 2, CT // 2)
            pe.wait_ge(x_free, CT)
            pe.wait_ge(xn_ready, 1)
            turn(ps_x, xn[0], x_full)
            pe.wait_ge(x_free, CT + 1)
            pe.wait_ge(p_free, CT)
            split_product(ps_s, xt_buf, m_buf, s_full)
            pe.wait_ge(xn_ready, 2)
            turn(ps_x, xn[1], x_full)

            with pe.Fori(0, B - 1) as b:
                with pe.Fori(0, TB // 2 - 1) as j:
                    step(b, 2 * j, 0, b * TB + 2 * j)
                    step(b, 2 * j + 1, 1, b * TB + 2 * j + 1)
                step(b, TB - 2, 0, b * TB + TB - 2)
                step(b, TB - 1, 1, b * TB + TB - 1, first_m=True)
            with pe.Fori(0, TB // 2 - 1) as j:
                step(B - 1, 2 * j, 0, (B - 1) * TB + 2 * j)
                step(B - 1, 2 * j + 1, 1, (B - 1) * TB + 2 * j + 1)
            step(B - 1, TB - 2, 0, T - 2, x_next=False)
            step(B - 1, TB - 1, 1, T - 1, scores=False, x_next=False)

            pe.wait_ge(x_free, x_uses(B - 1, TB - 2))
            pe.wait_ge(p_free, p_uses(B - 1, TB))
            for a in range(CT):
                pe.wait_ge(w8_ready, a + 1)
                if a >= 2:
                    pe.wait_ge(w8_read, a - 1)
                for c in range(CT):
                    mm = nc.tensor.transpose(w8_ps[a % 2][:, c * P:(c + 1) * P], w8_q[:, a, c * P:(c + 1) * P],
                                             ident_bf[:])
                mm.then_inc(w8_full, 1)

            def turn_r(t, e, first):
                pe.wait_ge(r_ready, t + 1)
                if not first:
                    pe.wait_ge(rt_ready, t - 1)
                for c in range(CT):
                    mm = nc.tensor.transpose(r_ps[e][:, c * P:(c + 1) * P], r_t[e][:, c * P:(c + 1) * P], ident_bf[:])
                mm.then_inc(r_full, 1)

            def linear(t, e, first):
                pe.wait_ge(rt_ready, t + 1)
                if not first:
                    pe.wait_ge(y_ready, t - 1)
                for c in range(CT):
                    for half in range(2):
                        cols = slice(half * HALF, (half + 1) * HALF)
                        mm = nc.tensor.matmul(y_ps[e][:, cols], rt_t[e][:, c * P:(c + 1) * P], w8_t[:, c, cols],
                                              start=(c == 0), stop=(c == CT - 1))
                mm.then_inc(y_full, 1)

            pe.wait_ge(w8_read, CT)
            pe.wait_ge(x1_ready, T)
            turn_r(0, 0, True)
            turn_r(1, 1, True)
            linear(0, 0, True)
            turn_r(2, 0, False)
            linear(1, 1, True)
            with pe.Fori(1, T // 2 - 1) as j:
                turn_r(2 * j + 1, 1, False)
                linear(2 * j, 0, False)
                turn_r(2 * j + 2, 0, False)
                linear(2 * j + 1, 1, False)
            turn_r(T - 1, 1, False)
            linear(T - 2, 0, False)
            linear(T - 1, 1, False)

        @block.scalar
        def _(act):
            n = 0
            for n in range(USES_CTX + USES_WKV):
                act.wait_ge(turned, n + 1)
                if n == 0:
                    to = ctx_t
                else:
                    to = wkv_t[:, :, (n - 1) * HALF:n * HALF]
                nc.scalar.activation(to, slots0[n % 4][:].rearrange("p (a k) -> p a k", a=LT), ACT.Copy).then_inc(turned_read, 1)
            for g2 in range(USES_KV):
                n = USES_CTX + USES_WKV + g2
                act.wait_ge(turned, n + 1)
                nc.scalar.activation(kv_f[:, 2 * g2:2 * g2 + 2, :], slots0[n % 4][:].rearrange("p (a k) -> p a k", a=2),
                                     ACT.Copy).then_inc(turned_read, 1)
            act.wait_ge(scales_made, 1)
            for i, col in ((0, 2), (1, 3)):
                part = slice(i * NP, (i + 1) * NP)
                nc.scalar.activation(kv_hi[:, part, :], kv_f[:, part, :], ACT.Copy, scale=to_f16[:, col:col + 1]).then_inc(act_hi0, 1)
            act.wait_ge(kv_stored, 16 * 8 * B)
            for h in range(0, NH, 4):
                nc.scalar.activation(wq_stack[:, h:h + 4, :], wq_f[h // NP][:, h % NP:h % NP + 4, :], ACT.Copy,
                                     scale=to_f16[:, 0:1]).then_inc(act_hi0, 1)
            for j in range(NP):
                n = USES_CTX + USES_WKV + USES_KV + j
                act.wait_ge(turned, n + 1)
                nc.scalar.activation(wo_t[:, 0, j, :], slots0[n % 4][:], ACT.Copy, scale=to_f16[:, 1:2]).then_inc(act_hi0, 1)

            def take_hi(to, slot, full, n, scale, done):
                act.wait_ge(full, n)
                nc.scalar.activation(to, slot[:], ACT.Copy, scale=scale).then_inc(done, 1)

            def take_mn(x_before, p_before, to):
                for c in range(CT):
                    slot, full, done, before = ((ps_x, x_full, x_hi, x_before), (ps_p, p_full, p_hi, p_before))[c % 2]
                    take_hi(to[:, 0, c, :], slot, full, before + c // 2 + 1, MN_SCALE, done)

            def exponentials(t, free=True):
                act.wait_ge(s_read, t + 1)
                nc.scalar.activation(ex, sub, ACT.Exp, scale=score_scale[:]).then_inc(exp_done, 1)

            def deviations(t, e):
                act.wait_ge(mean_ready, t + 1)
                nc.scalar.activation(dev, x1[e], ACT.Abs, bias=neg_mean[e][:]).then_inc(dev_ready, 1)

            def step(b, tt, e, t, scores=True, x_next=True, first_m=False, first=False):
                xb, pb = x_uses(b, tt), p_uses(b, tt)
                take_hi(pt_buf[:, 0, :], ps_p, p_full, pb + 1, P_SCALE, p_hi)
                grown = 0
                if not first:
                    deviations(t - 1, 1 - e)
                if first_m:
                    take_mn(xb, pb + 1, m_buf)
                    grown = CT // 2
                if x_next:
                    take_hi(xt_buf[:, 0, :], ps_x, x_full, xb + grown + 1, XN_SCALE, x_hi)
                if scores:
                    exponentials(t + 1)
                if first_m:
                    take_mn(xb + grown + 1, pb + 1 + grown, n_buf)

            act.wait_ge(wq_ready, 1)
            take_mn(0, 0, m_buf)
            take_mn(CT // 2, CT // 2, n_buf)
            take_hi(xt_buf[:, 0, :], ps_x, x_full, CT + 1, XN_SCALE, x_hi)
            take_hi(xt_buf[:, 0, :], ps_x, x_full, CT + 2, XN_SCALE, x_hi)
            exponentials(0)
            step(0, 0, 0, 0, first=True)
            step(0, 1, 1, 1)
            with act.Fori(1, TB // 2 - 1) as j:
                step(0, 2 * j, 0, 2 * j)
                step(0, 2 * j + 1, 1, 2 * j + 1)
            step(0, TB - 2, 0, TB - 2)
            step(0, TB - 1, 1, TB - 1, first_m=True)
            with act.Fori(1, B - 1) as b:
                with act.Fori(0, TB // 2 - 1) as j:
                    step(b, 2 * j, 0, b * TB + 2 * j)
                    step(b, 2 * j + 1, 1, b * TB + 2 * j + 1)
                step(b, TB - 2, 0, b * TB + TB - 2)
                step(b, TB - 1, 1, b * TB + TB - 1, first_m=True)
            with act.Fori(0, TB // 2 - 1) as j:
                step(B - 1, 2 * j, 0, (B - 1) * TB + 2 * j)
                step(B - 1, 2 * j + 1, 1, (B - 1) * TB + 2 * j + 1)
            step(B - 1, TB - 2, 0, T - 2, x_next=False)
            step(B - 1, TB - 1, 1, T - 1, scores=False, x_next=False)
            deviations(T - 1, 1)

            for a in range(CT):
                act.wait_ge(w8_full, a + 1)
                nc.scalar.activation(w8_t[:, :, a * P:(a + 1) * P],
                                     w8_ps[a % 2].rearrange("p (c o) -> p c o", c=CT), ACT.Copy).then_inc(w8_read, 1)

            def values(t, i, e, first):
                act.wait_ge(got_x1[i], (t - i) * (16 // X2) + 16)
                if not first:
                    act.wait_ge(r_ready, t - 1)
                nc.scalar.activation(u_t[e], x2[i], ACT.Identity, bias=quant_b20[:, bass.ds(t, 1)],
                                     scale=quant_a20[:, bass.ds(t, 1)]).then_inc(v_ready, 1)
                nc.scalar.activation(v_t[e], x2[i], ACT.Identity, bias=quant_b[:, bass.ds(t, 1)],
                                     scale=quant_a[:, bass.ds(t, 1)]).then_inc(v_ready, 1)

            def copy_rt(t, e, first):
                act.wait_ge(r_full, t + 1)
                if not first:
                    act.wait_ge(y_full, t - 1)
                nc.scalar.activation(rt_t[e], r_ps[e], ACT.Copy).then_inc(rt_ready, 1)

            def scaled(t, e, first):
                act.wait_ge(y_full, t + 1)
                if not first:
                    act.wait_ge(sum_ready, t - 1)
                nc.scalar.activation(y_t[e], y_ps[e][:], ACT.Copy, scale=small[:, 8:9]).then_inc(y_ready, 1)

            act.wait_ge(quant_ready, 1)
            values(0, 0, 0, True)
            values(1, 1, 1, True)
            copy_rt(0, 0, True)
            values(2, 2, 0, False)
            copy_rt(1, 1, True)
            values(3, 3, 1, False)
            scaled(0, 0, True)
            copy_rt(2, 0, False)
            values(4, 4, 0, False)
            scaled(1, 1, True)
            copy_rt(3, 1, False)
            values(5, 5, 1, False)

            def step2(t, i):
                scaled(t, i % 2, False)
                copy_rt(t + 2, i % 2, False)
                values(t + 4, (i + 4) % X2, i % 2, False)

            for t in range(2, 4):
                step2(t, t)
            with act.Fori(0, T // X2 - 1) as q:
                for i in range(X2):
                    step2(q * X2 + 4 + i, (4 + i) % X2)
            for t in range(T - 4, T):
                scaled(t, t % 2, False)
                if t + 2 < T:
                    copy_rt(t + 2, t % 2, False)

        @block.vector
        def _(dve):
            steps = [0]

            def then(ins):
                steps[0] += 1
                ins.then_inc(dve_step, 1)
                dve.wait_ge(dve_step, steps[0])

            for half in range(2):
                dve.wait_ge(got_wq[half], 32)
                nc.vector.tensor_reduce(small[:, 4 + half:5 + half], wq_f[half], AX.XY, ALU.max,
                                        apply_absolute_value=True).then_inc(dve_step, 1)
            dve.wait_ge(got_wout, 32)
            nc.vector.tensor_reduce(amax4[:, 1:2], wout_f, AX.XY, ALU.max, apply_absolute_value=True).then_inc(dve_step, 1)
            dve.wait_ge(turned_read, USES_CTX + USES_WKV + USES_KV)
            for i, col in ((0, 2), (1, 3)):
                nc.vector.tensor_reduce(amax4[:, col:col + 1], kv_f[:, i * NP:(i + 1) * NP, :], AX.XY, ALU.max,
                                        apply_absolute_value=True).then_inc(dve_step, 1)
            steps[0] = 5
            dve.wait_ge(dve_step, steps[0])
            then(nc.vector.tensor_tensor(amax4[:, 0:1], small[:, 4:5], small[:, 5:6], ALU.max))
            nc.vector.tensor_scalar(small[:, 0:1], amax4[:, 0:1], 0.0, None, ALU.mult).then_inc(amax_rows, 1)
            dve.wait_ge(amax_done, 1)
            then(nc.vector.tensor_scalar(amax4_all[:], amax4_all[:], AMAX_FLOOR, None, ALU.max))
            then(nc.vector.tensor_scalar(amax4_all[:].bitcast(U32), amax4_all[:].bitcast(U32), EXPONENT_BITS, None,
                                         ALU.bitwise_and))
            then(nc.vector.tensor_scalar(from_f16[:], amax4_all[:], 1.0 / AMAX_TO, None, ALU.mult))
            then(nc.vector.reciprocal(to_f16[:], from_f16[:]))
            then(nc.vector.tensor_scalar(score_scale[:], from_f16[:, 0:1], from_f16[:, 2:3],
                                         1.0 / (MN_SCALE * XN_SCALE * HD ** 0.5), ALU.mult, ALU.mult))
            then(nc.vector.tensor_scalar(out_scale[:], from_f16[:, 1:2], from_f16[:, 3:4],
                                         1.0 / (MN_SCALE * P_SCALE), ALU.mult, ALU.mult))
            nc.vector.tensor_scalar(small[:, 0:1], out_scale[:], 1.0, None, ALU.mult).then_inc(scales_made, 1)
            for i, col in ((0, 2), (1, 3)):
                part = slice(i * NP, (i + 1) * NP)
                dve.wait_ge(act_hi0, i + 1)
                last = nc.vector.scalar_tensor_tensor(out=kv_lo[:, part, :], in0=kv_f[:, part, :],
                                                      scalar=to_f16[:, col:col + 1], in1=kv_hi[:, part, :],
                                                      op0=ALU.mult, op1=ALU.subtract)
                if i == 0:
                    last.then_inc(dve_step, 1)
            steps[0] += 1
            last.then_inc(kv_split, 1)
            low = slice(HD, P)
            for i, h in enumerate(range(0, NH, 4)):
                dve.wait_ge(act_hi0, 3 + i)
                nc.vector.scalar_tensor_tensor(out=wq_stack[low, h:h + 4, :], in0=wq_f[h // NP][low, h % NP:h % NP + 4, :],
                                               scalar=to_f16[low, 0:1], in1=wq_stack[low, h:h + 4, :],
                                               op0=ALU.mult, op1=ALU.subtract).then_inc(dve_step, 1)
            steps[0] += 4
            dve.wait_ge(dve_step, steps[0])
            nc.vector.tensor_scalar(small[:, 0:1], out_scale[:], 1.0, None, ALU.mult).then_inc(wq_ready, 1)
            for j in range(NP):
                n = USES_CTX + USES_WKV + USES_KV + j
                dve.wait_ge(act_hi0, 2 + NH // 4 + j + 1)
                nc.vector.scalar_tensor_tensor(out=wo_t[:, 1, j, :], in0=slots0[n % 4][:], scalar=to_f16[:, 1:2],
                                               in1=wo_t[:, 0, j, :], op0=ALU.mult,
                                               op1=ALU.subtract).then_inc(turned_read, 1)

            def take_lo(to, hi, slot, n, scale, hi_done, free):
                dve.wait_ge(hi_done, n)
                nc.vector.scalar_tensor_tensor(out=to, in0=slot[:], scalar=scale, in1=hi, op0=ALU.mult,
                                               op1=ALU.subtract).then_inc(free, 1)

            def take_mn(x_before, p_before, to):
                for c in range(CT):
                    slot, done, free, before = ((ps_x, x_hi, x_free, x_before), (ps_p, p_hi, p_free, p_before))[c % 2]
                    take_lo(to[:, 1, c, :], to[:, 0, c, :], slot, before + c // 2 + 1, MN_SCALE, done, free)

            def variance(t, e):
                dve.wait_ge(got_xa[e], (t - e) * 8 + 16)
                for half in range(2):
                    nc.vector.bn_stats(stats_a[:, half, :], xa[e][:, half * HALF:(half + 1) * HALF]).then_inc(a_stats, 1)
                dve.wait_ge(a_stats, 2 * t + 2)
                nc.vector.memset(wait_carrier[:], 0.0)
                nc.vector.bn_aggr(mv_a[e][:], stats_a[:].rearrange("p a b -> p (a b)")).then_inc(a_aggr, 1)
                dve.wait_ge(a_aggr, t + 1)
                nc.vector.tensor_scalar(veps[e][:], mv_a[e][:, 1:2], LN_EPS, None, ALU.add).then_inc(var_ready, 1)

            def normalise(t, e, first):
                dve.wait_ge(rstd_ready, t + 1)
                nc.vector.tensor_scalar(xn[e], xa[e], mv_a[e][:, 0:1], rstd[e][:], ALU.subtract,
                                        ALU.mult).then_inc(xn_ready, 1)

            def heads(ap):
                return ap.rearrange("p (h k) -> p h k", h=NH)

            def across(ap):
                return ap.unsqueeze(2).to_broadcast([P, NH, SK])

            def mask_scores(t):
                dve.wait_ge(s_full, t + 1)
                nc.vector.tensor_tensor(heads(ps_s[:]), heads(ps_s[:]),
                                        causal[:].unsqueeze(1).to_broadcast([P, NH, SK]), ALU.add).then_inc(masked, 1)

            def maxima(t, masks=None):
                if masks is None:
                    dve.wait_ge(s_full, t + 1)
                else:
                    dve.wait_ge(masked, masks)
                nc.vector.tensor_reduce(hmax[:], heads(ps_s[:]), AX.X, ALU.max).then_inc(max_done, 1)
                dve.wait_ge(max_done, t + 1)
                nc.vector.tensor_tensor(heads(sub), heads(ps_s[:]), across(hmax[:]), ALU.subtract).then_inc(s_read, 1)

            def probabilities(t):
                dve.wait_ge(exp_done, t + 1)
                nc.vector.tensor_reduce(hsum[:], heads(ex), AX.X, ALU.add).then_inc(sum_done, 1)
                dve.wait_ge(sum_done, t + 1)
                nc.vector.reciprocal(hinv[:], hsum[:]).then_inc(inv_done, 1)
                dve.wait_ge(inv_done, t + 1)
                nc.vector.tensor_tensor(heads(pr), heads(ex), across(hinv[:]), ALU.mult).then_inc(p_ready, 1)

            def residual(t, e, stored=True):
                dve.wait_ge(o_full, t + 1)
                dve.wait_ge(got_xr[e], (t - e) * 8 + 16)
                if stored:
                    dve.wait_ge(x1_stored[e], (t - e) * 8)
                nc.vector.scalar_tensor_tensor(out=x1[e], in0=ps_o[:], scalar=out_scale[:], in1=xr[e], op0=ALU.mult,
                                               op1=ALU.add).then_inc(x1_ready, 1)
                dve.wait_ge(x1_ready, t + 1)
                for half in range(2):
                    nc.vector.bn_stats(stats_b[:, half, :], x1[e][:, half * HALF:(half + 1) * HALF]).then_inc(b_stats, 1)
                dve.wait_ge(b_stats, 2 * t + 2)
                nc.vector.memset(wait_carrier[:], 0.0)
                nc.vector.bn_aggr(mv_b[:], stats_b[:].rearrange("p a b -> p (a b)")).then_inc(b_aggr, 1)
                dve.wait_ge(b_aggr, t + 1)
                nc.vector.tensor_scalar(neg_mean[e][:], mv_b[:, 0:1], -1.0, None, ALU.mult).then_inc(mean_ready, 1)
                nc.vector.tensor_copy(mean1[:, bass.ds(t, 1)], mv_b[:, 0:1]).then_inc(kept, 1)
                nc.vector.tensor_scalar(var1[:, bass.ds(t, 1)], mv_b[:, 1:2], LN_EPS, None, ALU.add).then_inc(kept, 1)

            def peak(t):
                dve.wait_ge(dev_ready, t + 1)
                nc.vector.tensor_reduce(peak1[:, bass.ds(t, 1)], dev, AX.X, ALU.max).then_inc(x1_done, 1)

            def step(b, tt, e, t, scores=True, x_next=True, first_m=False, first=False, norm=True):
                xb, pb = x_uses(b, tt), p_uses(b, tt)
                take_lo(pt_buf[:, 1, :], pt_buf[:, 0, :], ps_p, pb + 1, P_SCALE, p_hi, p_free)
                if not first:
                    residual(t - 1, 1 - e, stored=not (isinstance(t, int) and t < 3))
                grown = 0
                if first_m:
                    take_mn(xb, pb + 1, m_buf)
                    grown = CT // 2
                if norm:
                    variance(t + 3, 1 - e)
                if not first:
                    peak(t - 1)
                if norm:
                    normalise(t + 3, 1 - e, False)
                if scores:
                    if first_m:
                        mask_scores(t + 1)
                        maxima(t + 1, masks=b + 2)
                    else:
                        maxima(t + 1)
                if x_next:
                    take_lo(xt_buf[:, 1, :], xt_buf[:, 0, :], ps_x, xb + grown + 1, XN_SCALE, x_hi, x_free)
                if scores:
                    probabilities(t + 1)
                if first_m:
                    take_mn(xb + grown + 1, pb + 1 + grown, n_buf)

            dve.wait_ge(turned_read, USES0)
            variance(0, 0)
            variance(1, 1)
            take_mn(0, 0, m_buf)
            normalise(0, 0, True)
            normalise(1, 1, True)
            take_mn(CT // 2, CT // 2, n_buf)
            take_lo(xt_buf[:, 1, :], xt_buf[:, 0, :], ps_x, CT + 1, XN_SCALE, x_hi, x_free)
            variance(2, 0)
            mask_scores(0)
            maxima(0, masks=1)
            take_lo(xt_buf[:, 1, :], xt_buf[:, 0, :], ps_x, CT + 2, XN_SCALE, x_hi, x_free)
            normalise(2, 0, False)
            probabilities(0)
            step(0, 0, 0, 0, first=True)
            step(0, 1, 1, 1)
            step(0, 2, 0, 2)
            step(0, 3, 1, 3)
            step(0, 4, 0, 4)
            step(0, 5, 1, 5)
            step(0, 6, 0, 6)
            step(0, 7, 1, 7, first_m=True)
            with dve.Fori(1, B - 1) as b:
                with dve.Fori(0, TB // 2 - 1) as j:
                    step(b, 2 * j, 0, b * TB + 2 * j)
                    step(b, 2 * j + 1, 1, b * TB + 2 * j + 1)
                step(b, TB - 2, 0, b * TB + TB - 2)
                step(b, TB - 1, 1, b * TB + TB - 1, first_m=True)
            for tt in range(TB):
                t = (B - 1) * TB + tt
                step(B - 1, tt, tt % 2, t, norm=t + 3 < T, x_next=t + 2 < T, scores=t + 1 < T)
            residual(T - 1, 1)
            peak(T - 1)

            dve.wait_ge(kept, 2 * T)
            nc.vector.tensor_copy(small[:, 15:16], mv_b[:, 0:1]).then_inc(var1_ready, 1)

            dve.wait_ge(got_w8, 16)
            nc.vector.tensor_reduce(small[:, 0:1], w8_raw, AX.XY, ALU.max, apply_absolute_value=True).then_inc(w_amax_rows, 1)
            chain = [0]

            def then2(ins):
                chain[0] += 1
                ins.then_inc(chain2, 1)
                dve.wait_ge(chain2, chain[0])

            dve.wait_ge(rstd1_ready, 1)
            dve.wait_ge(x1_done, T)
            then2(nc.vector.tensor_tensor(quant_a20[:], peak1[:], rstd1[:], ALU.mult))
            nc.vector.tensor_reduce(small[:, 2:3], quant_a20[:], AX.X, ALU.max).then_inc(x_amax_rows, 1)
            dve.wait_ge(w_amax_done, 1)
            then2(nc.vector.tensor_scalar(small[:, 4:5], small[:, 1:2], 1.0 / E4M3_MAX, 1e-12, ALU.mult, ALU.max))
            then2(nc.vector.reciprocal(small[:, 5:6], small[:, 4:5]))

            def round_e4m3(rounded, v, u, g, s):
                then2(nc.vector.tensor_scalar(g.bitcast(U32), u.bitcast(U32), EXPONENT_BITS, HALF_BIT,
                                              ALU.bitwise_and, ALU.bitwise_or))
                then2(nc.vector.scalar_tensor_tensor(out=s, in0=g, scalar=ROUND_LEAST, in1=v, op0=ALU.max, op1=ALU.add))
                return nc.vector.scalar_tensor_tensor(out=rounded, in0=g, scalar=ROUND_LEAST, in1=s, op0=ALU.max,
                                                      op1=ALU.subtract)

            SPLIT16 = 2.0 ** 8 + 1.0
            for a in range(CT):
                w, s, v, u = w_tmp
                then2(nc.vector.tensor_scalar(w, w8_raw[:, a, :], small[:, 5:6], None, ALU.mult))
                then2(nc.vector.scalar_tensor_tensor(out=s, in0=w, scalar=SPLIT16, in1=w, op0=ALU.mult, op1=ALU.subtract))
                then2(nc.vector.scalar_tensor_tensor(out=v, in0=w, scalar=SPLIT16, in1=s, op0=ALU.mult, op1=ALU.subtract))
                then2(nc.vector.tensor_scalar(u, v, ROUND_SHIFT, None, ALU.mult))
                round_e4m3(w8_q[:, a, :], v, u, w, s).then_inc(w8_ready, 1)
                dve.wait_ge(w8_ready, a + 1)

            dve.wait_ge(x_amax_done, 1)
            then2(nc.vector.tensor_scalar(small[:, 6:7], small[:, 3:4], 1.0 / E4M3_MAX, 1e-12, ALU.mult, ALU.max))
            then2(nc.vector.reciprocal(small[:, 7:8], small[:, 6:7]))
            then2(nc.vector.tensor_scalar(small[:, 8:9], small[:, 6:7], small[:, 4:5], None, ALU.mult))
            then2(nc.vector.tensor_scalar(quant_a[:], rstd1[:], small[:, 7:8], None, ALU.mult))
            then2(nc.vector.scalar_tensor_tensor(out=quant_b[:], in0=mean1[:], scalar=-1.0, in1=quant_a[:], op0=ALU.mult,
                                                 op1=ALU.mult))
            then2(nc.vector.tensor_scalar(quant_a20[:], quant_a[:], ROUND_SHIFT, None, ALU.mult))
            nc.vector.tensor_scalar(quant_b20[:], quant_b[:], ROUND_SHIFT, None, ALU.mult).then_inc(quant_ready, 1)

            def rounding(t, e, first):
                if not (isinstance(t, int) and t == 0):
                    dve.wait_ge(r_ready, t)
                dve.wait_ge(v_ready, 2 * t + 1)
                nc.vector.tensor_scalar(g_t.bitcast(U32), u_t[e].bitcast(U32), EXPONENT_BITS, HALF_BIT,
                                        ALU.bitwise_and, ALU.bitwise_or).then_inc(g_done, 1)
                dve.wait_ge(g_done, t + 1)
                dve.wait_ge(v_ready, 2 * t + 2)
                nc.vector.scalar_tensor_tensor(out=a_t, in0=g_t, scalar=ROUND_LEAST, in1=v_t[e], op0=ALU.max,
                                               op1=ALU.add).then_inc(a_done, 1)
                dve.wait_ge(a_done, t + 1)
                if not first:
                    dve.wait_ge(r_full, t - 1)
                nc.vector.scalar_tensor_tensor(out=r_t[e], in0=g_t, scalar=ROUND_LEAST, in1=a_t, op0=ALU.max,
                                               op1=ALU.subtract).then_inc(r_ready, 1)

            rounding(0, 0, True)
            rounding(1, 1, True)
            with dve.Fori(1, T // 2) as j:
                rounding(2 * j, 0, False)
                rounding(2 * j + 1, 1, False)


_INS = ['x', 'ctx_512', 'L0_xattn_Wq', 'L0_xattn_Wkv_expand', 'L0_xattn_Wout', 'L0_ffn_weight']
_OUTS = [((8, 1024, 1024), 'float32')]


def kernel(**inputs):
    import numpy as _np
    import concourse.bacc as _bacc
    from concourse import mybir as _mybir
    from concourse.bass_utils import run_bass_kernel_spmd as _run

    nc = _bacc.Bacc("TRN2", target_bir_lowering=False, num_devices=1)
    arrays, args = {}, []
    for name in _INS:
        a = _np.ascontiguousarray(inputs[name])
        arrays[f"in_{name}_dram"] = a
        args.append(nc.dram_tensor(f"in_{name}_dram", a.shape, _mybir.dt.from_np(a.dtype), kind="ExternalInput").ap())
    for i, (shape, dtype) in enumerate(_OUTS):
        dt = _mybir.dt.from_np(_np.dtype(dtype))
        args.append(nc.dram_tensor(f"out_{i}_dram", shape, dt, kind="ExternalOutput").ap())
    xattn_ffn_kernel(nc, *args)
    r = _run(nc, [arrays], core_ids=[0])
    return r.results[0]["out_0_dram"]
```

```python
from contextlib import ExitStack

import concourse.bass as bass
from concourse import mybir

F32 = mybir.dt.float32
F16 = mybir.dt.float16
BF16 = mybir.dt.bfloat16
U32 = mybir.dt.uint32
ALU = mybir.AluOpType
ACT = mybir.ActivationFunctionType
AX = mybir.AxisListType
ROWS_MAX = bass.bass_isa.ReduceOp.max

P = 128
HD = 64
LN_EPS = 1e-5
E4M3_MAX = 448.0

AMAX_TO = 2.0 ** 13
M_SCALE = 2.0 ** -20
N_SCALE = 2.0 ** -14
XN_SCALE = 2.0 ** 10
P_SCALE = 2.0 ** 14
AMAX_FLOOR = 2.0 ** -40
ROUND_SHIFT = 2.0 ** 20
ROUND_LEAST = 1.5 * 2.0 ** 14
EXPONENT_BITS = 0x7F800000
HALF_BIT = 0x00400000
MASKED = -3.0e38


def xattn_ffn_kernel(nc, x, ctx, Wq, Wkv, Wout, Wffn, out):
    B, S, H = x.shape
    SK, L = ctx.shape[1:]
    NH = H // HD
    NP = NH // 2
    CT = H // P
    LT = L // P
    TB = S // P
    T = B * TB
    KEYS = B * SK
    HALF = 512
    assert SK == HD and NP == CT and KEYS == HALF and TB == 8

    x_rows = x.rearrange("b s h -> (b s) h")
    out_rows = out.rearrange("b s h -> (b s) h")

    with ExitStack() as scope:
        def sb(name, shape, dt):
            return scope.enter_context(nc.sbuf_tensor(name, shape, dt))

        def sem(name):
            return scope.enter_context(nc.semaphore(name))

        x1_dram = nc.dram_tensor("x1_scratch", [T * P, H], F32, kind="Internal").ap()
        kv_dram = nc.dram_tensor("kv_scratch", [2, P, 2 * NP, KEYS], F16, kind="Internal").ap()

        wq_stack = sb("wq_stack", [P, NH, H], F16)
        wo_t = sb("wo_t", [P, 2, NP, H], F16)
        m_buf = sb("m_buf", [P, 2, CT, H], F16)
        n_buf = sb("n_buf", [P, 2, NP, H], F16)
        k_hilo = sb("k_hilo", [P, NH, SK], F16)
        k_lohi = sb("k_lohi", [P, NH, SK], F16)
        v_diag = sb("v_diag", [P, 2, NP, P], F16)

        w8_raw = sb("w8_raw", [P, CT, H], BF16)

        tile_space = sb("tile_space", [P, 13, H], F32)
        xa = [tile_space[:, i, :] for i in (0, 1)]
        xr = [tile_space[:, i, :] for i in (2, 3)]
        xn = [tile_space[:, i, :] for i in (4, 5)]
        x1 = [tile_space[:, i, :] for i in (6, 7)]
        sub = tile_space[:, 8, :]
        ex = tile_space[:, 9, :]
        dev = ex
        pr = tile_space[:, 10, :]
        xt_buf = tile_space[:, 11, :].bitcast(F16).rearrange("p (s n) -> p s n", s=2)
        pt_buf = tile_space[:, 12, :].bitcast(F16).rearrange("p (s n) -> p s n", s=2)

        ident = sb("ident", [P, P], F32)
        ident_bf = sb("ident_bf", [P, P], BF16)
        causal = sb("causal", [P, SK], F32)
        minus_half = sb("minus_half", [P, T], F32)
        amax4 = sb("amax4", [P, 4], F32)
        wout_sums = sb("wout_sums", [P, CT], F32)
        amax4_all = sb("amax4_all", [P, 4], F32)
        to_f16 = sb("to_f16", [P, 4], F32)
        from_f16 = sb("from_f16", [P, 4], F32)
        score_scale = sb("score_scale", [P, 1], F32)
        out_scale = sb("out_scale", [P, 1], F32)
        small = sb("small", [P, 16], F32)
        stats_a = sb("stats_a", [P, 2, 6], F32)
        stats_b = sb("stats_b", [P, 2, 6], F32)
        mv_a = [sb(f"mv_a{i}", [P, 2], F32) for i in (0, 1)]
        mv_b = sb("mv_b", [P, 2], F32)
        veps = [sb(f"veps_x{i}", [P, 1], F32) for i in (0, 1)]
        rstd = [sb(f"rstd_x{i}", [P, 1], F32) for i in (0, 1)]
        neg_mean = [sb(f"neg_mean{i}", [P, 1], F32) for i in (0, 1)]
        wait_carrier = sb("wait_carrier", [P, 1], F32)
        hmax = sb("hmax", [P, NH], F32)
        hsum = sb("hsum", [P, NH], F32)
        hinv = sb("hinv", [P, NH], F32)
        mean1 = sb("mean1", [P, T], F32)
        var1 = sb("var1", [P, T], F32)
        rstd1 = sb("rstd1", [P, T], F32)
        peak1 = sb("peak1", [P, T], F32)
        quant_a = sb("quant_a", [P, T], F32)
        quant_b = sb("quant_b", [P, T], F32)
        quant_a20, quant_b20 = ident[:, 0:T], ident[:, T:2 * T]

        ps_s = scope.enter_context(nc.psum_tensor("ps_s", [P, H], F32))
        ps_o = scope.enter_context(nc.psum_tensor("ps_o", [P, H], F32))
        ps_x = scope.enter_context(nc.psum_tensor("ps_x", [P, H], F32))
        ps_p = scope.enter_context(nc.psum_tensor("ps_p", [P, H], F32))

        def flat(t):
            return t[:].rearrange("p a b c -> p (a b c)")

        wq_f = flat(m_buf).bitcast(F32).rearrange("p (j c) -> p j c", c=H)
        wout_f = flat(n_buf).bitcast(F32).rearrange("p (a c) -> p a c", c=H)
        wkv_f = tile_space[:, 8:12, :].rearrange("p a (b l) -> p (a b) l", l=L)
        ctx_f = tile_space[:, 12, :].rearrange("p (a l) -> p a l", l=L)
        wkv_t = tile_space[:, 4:8, :].rearrange("p (a q) r -> p a (q r)", a=LT)
        ctx_t = tile_space[:, 3, :].rearrange("p (a k) -> p a k", a=LT)
        k_f = wo_t[:, 0].rearrange("p j c -> p (j c)").bitcast(F32).rearrange("p (j k) -> p j k", k=KEYS)
        v_f = w8_raw[:].rearrange("p j c -> p (j c)").bitcast(F32).rearrange("p (j k) -> p j k", k=KEYS)
        k_hi_t, k_lo_t = (tile_space[:, i:i + 2, :].rearrange("p a c -> p (a c)").bitcast(F16)
                          .rearrange("p (j k) -> p j k", k=KEYS) for i in (8, 10))
        v_hi_t, v_lo_t = (flat(n_buf)[:, i:i + 4096].rearrange("p (j k) -> p j k", k=KEYS) for i in (0, 4096))
        wq_nat_hi = wo_t[:, 0]
        wq_nat_lo = (tile_space[:, 4:8, :].rearrange("p a c -> p (a c)").bitcast(F16)
                     .rearrange("p (j c) -> p j c", c=H))
        NG = 2 * NP
        EVEN, ODD = slice(0, HD), slice(HD, P)

        def wq_heads(e):
            return wq_stack[:].rearrange("p (j e) c -> p e j c", e=2)[:, e]

        const_made = sem("const_made")
        diag_zeroed = sem("diag_zeroed")
        got_ctx = sem("got_ctx")
        got_wkv = [sem(f"got_wkv{q}") for q in range(4)]
        got_wq = [sem(f"got_wq{i}") for i in range(2)]
        got_wout = [sem(f"got_wout{i}") for i in range(2)]
        turned = sem("turned")
        turned_read = sem("turned_read")
        wt_full = sem("wt_full")
        wt_hi = sem("wt_hi")
        wt_free = sem("wt_free")
        wout_sum = sem("wout_sum")
        amax_rows = sem("amax_rows")
        amax_done = sem("amax_done")
        scales_made = sem("scales_made")
        dve_step = sem("dve_step")
        k_hi = sem("k_hi")
        v_hi = sem("v_hi")
        wq_hi = sem("wq_hi")
        k_split = sem("k_split")
        v_split = sem("v_split")
        wq_split = sem("wq_split")
        wq_moved = sem("wq_moved")
        kv_stored = sem("kv_stored")
        got_k = sem("got_k")
        got_v = sem("got_v")
        got_xa = [sem("got_xa0"), sem("got_xa1")]
        got_xr = [sem("got_xr0"), sem("got_xr1")]
        var_ready = sem("var_ready")
        rstd_ready = sem("rstd_ready")
        xn_ready = sem("xn_ready")
        x_full = sem("x_full")
        x_hi = sem("x_hi")
        x_free = sem("x_free")
        p_full = sem("p_full")
        p_hi = sem("p_hi")
        p_free = sem("p_free")
        s_full = sem("s_full")
        s_read = sem("s_read")
        exp_done = sem("exp_done")
        p_ready = sem("p_ready")
        o_full = sem("o_full")
        x1_ready = sem("x1_ready")
        a_stats = sem("a_stats")
        a_aggr = sem("a_aggr")
        b_stats = sem("b_stats")
        b_aggr = sem("b_aggr")
        masked = sem("masked")
        max_done = sem("max_done")
        sum_done = sem("sum_done")
        inv_done = sem("inv_done")
        kept = sem("kept")
        mean_ready = sem("mean_ready")
        dev_ready = sem("dev_ready")
        x1_done = sem("x1_done")
        x1_stored = [sem("x1_stored0"), sem("x1_stored1")]
        var1_ready = sem("var1_ready")
        rstd1_ready = sem("rstd1_ready")
        got_w8 = sem("got_w8")
        w_amax_rows = sem("w_amax_rows")
        w_amax_done = sem("w_amax_done")
        w_scale_made = sem("w_scale_made")
        w_quot = sem("w_quot")
        x_amax_rows = sem("x_amax_rows")
        x_amax_done = sem("x_amax_done")
        w8_ready = sem("w8_ready")
        w8_full = sem("w8_full")
        w8_read = sem("w8_read")
        quant_ready = sem("quant_ready")
        g_done = sem("g_done")
        a_done = sem("a_done")
        got_x1 = [sem(f"got_x1_{i}") for i in range(8)]
        u_ready = sem("u_ready")
        v_ready = sem("v_ready")
        v_odd = sem("v_odd")
        r_ready = sem("r_ready")
        r_full = sem("r_full")
        rt_ready = sem("rt_ready")
        y_full = sem("y_full")
        y_ready = sem("y_ready")
        sum_ready = sem("sum_ready")
        out_stored = [sem(f"out_stored{i}") for i in range(8)]

        wq_flat = wq_stack[:].rearrange("p h c -> p (h c)")
        w_tmp = [wq_flat[:, i * 2048:(i + 1) * 2048].bitcast(F32) for i in range(4)]
        w8_q = [wq_flat[:, 8192 + i * H:8192 + (i + 1) * H].bitcast(BF16) for i in range(2)]
        w8_t = wo_t[:, 0].bitcast(BF16)
        w8_ps = ps_p[:, 0:HALF].bitcast(BF16)
        X2 = 8
        x2 = [tile_space[:, i, :] for i in range(X2)]
        flat_n = flat(n_buf)
        v_t, u_t, g_t, a_t = ([flat_n[:, i * 2048:(i + 1) * 2048].bitcast(F32) for i in (k, k + 1)] for k in (0, 2, 4, 6))
        r_t = [tile_space[:, 10, :].bitcast(BF16)[:, i * H:(i + 1) * H] for i in (0, 1)]
        rt_t = [tile_space[:, 11, :].bitcast(BF16)[:, i * H:(i + 1) * H] for i in (0, 1)]
        y_t = [tile_space[:, 12, :].bitcast(BF16)[:, i * H:(i + 1) * H] for i in (0, 1)]
        r_ps = [ps_x[:, 0:HALF].bitcast(BF16), ps_p[:, 0:HALF].bitcast(BF16)]
        y_ps = [ps_s, ps_o]

        slots0 = [ps_s, ps_o, ps_x, ps_p]
        USES_CTX, USES_WKV, USES_KV = 1, 4, NG // 2
        USES0 = USES_CTX + USES_WKV + USES_KV

        def is_step(tt, n):
            return isinstance(tt, int) and tt == n

        QUAD = CT // 2

        def extra(b, tt):
            if not isinstance(tt, int):
                return QUAD
            return QUAD * ((tt > 0) + (tt > TB - 2 and not is_step(b, B - 1)))

        def x_uses(b, tt):
            return b * (TB + CT) + tt + (QUAD + 2 + extra(b, tt))

        def p_uses(b, tt):
            return b * (TB + CT) + tt + (QUAD + extra(b, tt))

        PASSES = ((0, 0), (0, 1), (1, 0))

        block = scope.enter_context(nc.Block())

        def batch(eng, b, step, unroll=False):
            step(b, 0, 0, b * TB)
            if unroll:
                for tt in range(1, 5):
                    step(b, tt, tt % 2, b * TB + tt)
            else:
                with eng.Fori(0, 2) as j:
                    step(b, 2 * j + 1, 1, b * TB + 2 * j + 1)
                    step(b, 2 * j + 2, 0, b * TB + 2 * j + 2)
            for tt in range(5, TB):
                step(b, tt, tt % 2, b * TB + tt)

        @block.sync
        def _(sp):
            sp.dma_start(ctx_f, ctx.rearrange("b k l -> (b k) l").rearrange("(a p) l -> p a l", p=P)).then_inc(got_ctx, 16)
            wkv_rows = Wkv.rearrange("(a p) l -> p a l", p=P)
            for q in range(4):
                sp.dma_start(wkv_f[:, 4 * q:4 * q + 4, :], wkv_rows[:, 4 * q:4 * q + 4, :]).then_inc(got_wkv[q], 16)
            wq_rows = Wq.rearrange("(j p) c -> p j c", p=P)
            wout_rows = Wout.rearrange("(a p) c -> p a c", p=P)
            for i in range(2):
                half = slice(4 * i, 4 * i + 4)
                sp.dma_start(wq_f[:, half, :], wq_rows[:, half, :]).then_inc(got_wq[i], 16)
            for i in range(2):
                half = slice(4 * i, 4 * i + 4)
                sp.dma_start(wout_f[:, half, :], wout_rows[:, half, :]).then_inc(got_wout[i], 16)

            def load_x(to, got, t, e):
                sp.dma_start(to[e], x_rows[bass.ds(t * P, P), :]).then_inc(got[e], 16)

            load_x(xa, got_xa, 0, 0)
            load_x(xa, got_xa, 1, 1)
            load_x(xr, got_xr, 0, 0)

            def load_k(of):
                for to, swap in ((k_hilo, 0), (k_lohi, 1)):
                    for s, rows in enumerate((EVEN, ODD)):
                        for e in range(2):
                            sp.dma_start(to[rows].rearrange("d (j e) k -> d e j k", e=2)[:, e],
                                         of(s ^ swap, e)).then_inc(got_k, 16)

            def load_v(of):
                for s in range(2):
                    for rows in (EVEN, ODD):
                        sp.dma_start(v_diag[rows, s, :, rows], of(s, rows)).then_inc(got_v, 16)

            sp.wait_ge(k_split, 1)
            load_k(lambda s, e: (k_hi_t, k_lo_t)[s][(EVEN, ODD)[e], :, 0:SK])
            for i in range(4):
                sp.wait_ge(wq_split, i + 1)
                pairs = slice(2 * i, 2 * i + 2)
                for src, even_to, odd_to in ((wq_nat_hi, EVEN, ODD), (wq_nat_lo, ODD, EVEN)):
                    sp.dma_start(wq_heads(0)[even_to, pairs, :], src[EVEN, pairs, :]).then_inc(wq_moved, 16)
                    sp.dma_start(wq_heads(1)[odd_to, pairs, :], src[ODD, pairs, :]).then_inc(wq_moved, 16)
            for s, src in enumerate((k_hi_t, k_lo_t)):
                sp.dma_start(kv_dram[s, :, 0:NP, :], src).then_inc(kv_stored, 16)
            sp.wait_ge(diag_zeroed, 1)
            sp.wait_ge(v_split, 1)
            load_v(lambda s, rows: (v_hi_t, v_lo_t)[s][rows, :, 0:SK])
            for s, src in enumerate((v_hi_t, v_lo_t)):
                sp.dma_start(kv_dram[s, :, NP:NG, :], src).then_inc(kv_stored, 16)
            sp.dma_start(w8_raw[:], Wffn.rearrange("(a p) c -> p a c", p=P)).then_inc(got_w8, 16)
            for t in range(2, 4):
                sp.wait_ge(xn_ready, t - 1)
                load_x(xa, got_xa, t, t % 2)

            def next_kv(b):
                sp.wait_ge(p_full, p_uses(b - 1, 0))
                if isinstance(b, int):
                    sp.wait_ge(kv_stored, 64)
                load_k(lambda s, e: kv_dram[s, (EVEN, ODD)[e], 0:NP, bass.ds(b * SK, SK)])
                sp.wait_ge(p_full, p_uses(b - 1, 1))
                load_v(lambda s, rows: kv_dram[s, rows, NP:NG, bass.ds(b * SK, SK)])

            def step(b, tt, e, t):
                known = isinstance(t, int)
                if not known or t + 4 < T:
                    sp.wait_ge(xn_ready, t + 3)
                    load_x(xa, got_xa, t + 4, e)
                if not (known and t == 0):
                    sp.wait_ge(x1_ready, t + 1)
                if not known or t + 1 < T:
                    load_x(xr, got_xr, t + 1, 1 - e)
                if not (known and t == 0):
                    sp.dma_start(x1_dram[bass.ds((t - 1) * P, P), :], x1[1 - e]).then_inc(x1_stored[1 - e], 16)
                if is_step(tt, 0) and not (known and t >= T - TB):
                    next_kv(b + 1)

            batch(sp, 0, step)
            with sp.Fori(1, B - 1) as b:
                batch(sp, b, step)
            batch(sp, B - 1, step, unroll=True)
            sp.wait_ge(x1_ready, T + 1)
            sp.dma_start(x1_dram[(T - 1) * P:T * P, :], x1[(T - 1) % 2]).then_inc(x1_stored[(T - 1) % 2], 16)

            def load_x1(t, i):
                sp.dma_start(x2[i], x1_dram[bass.ds(t * P, P), :]).then_inc(got_x1[i], 16)

            for t in range(4):
                load_x1(t, t)
            for e in range(2):
                sp.wait_ge(x1_stored[e], 16 * (T // 2))
            sp.wait_ge(x1_done, T)
            for t in range(4, X2):
                load_x1(t, t)

            def store_out(t, i):
                sp.wait_ge(sum_ready, t + 1)
                sp.dma_start(out_rows[bass.ds(t * P, P), :], x2[i]).then_inc(out_stored[i], 16)

            with sp.Fori(0, T // X2 - 1) as q:
                for i in range(X2):
                    store_out(q * X2 + i, i)
                    if i % 2:
                        for k in (i - 1, i):
                            sp.wait_ge(out_stored[k], q * 16 + 16)
                            load_x1((q + 1) * X2 + k, k)
            for i in range(X2):
                store_out(T - X2 + i, i)
            for i in range(X2):
                sp.wait_ge(out_stored[i], 16 * (T // X2))
            sp.wait_ge(kv_stored, 64)

        @block.gpsimd
        def _(pool):
            nc.gpsimd.memset(ident[:], 0.0).then_inc(const_made, 1)
            nc.gpsimd.memset(causal[:], 0.0).then_inc(const_made, 1)
            nc.gpsimd.memset(minus_half[:], -0.5).then_inc(const_made, 1)
            pool.wait_ge(const_made, 3)
            nc.gpsimd.affine_select(out=ident[:], in_=ident[:], compare_op=ALU.not_equal, fill=1.0, base=0,
                                    pattern=[[-1, P]], channel_multiplier=1).then_inc(const_made, 1)
            nc.gpsimd.affine_select(out=causal[:], in_=causal[:], compare_op=ALU.is_ge, fill=MASKED, base=0,
                                    pattern=[[-1, SK]], channel_multiplier=1).then_inc(const_made, 1)
            pool.wait_ge(const_made, 5)
            nc.gpsimd.tensor_copy(ident_bf[:], ident[:]).then_inc(const_made, 1)
            nc.gpsimd.memset(flat(v_diag), 0.0).then_inc(diag_zeroed, 1)
            pool.wait_ge(amax_rows, 1)
            nc.gpsimd.partition_all_reduce(amax4_all[:, 0:2], amax4[:, 0:2], P, ROWS_MAX).then_inc(amax_done, 1)

            def inverse_deviation(t, e):
                pool.wait_ge(var_ready, t + 1)
                nc.gpsimd.tensor_tensor(rstd[e][:], veps[e][:], minus_half[:, 0:1], ALU.pow).then_inc(rstd_ready, 1)

            inverse_deviation(0, 0)
            inverse_deviation(1, 1)
            pool.wait_ge(amax_rows, 2)
            nc.gpsimd.partition_all_reduce(amax4_all[:, 2:4], amax4[:, 2:4], P, ROWS_MAX).then_inc(amax_done, 1)
            with pool.Fori(1, TB // 2) as j:
                inverse_deviation(2 * j, 0)
                inverse_deviation(2 * j + 1, 1)
            pool.wait_ge(w_amax_rows, 1)
            nc.gpsimd.partition_all_reduce(small[:, 1:2], small[:, 0:1], P, ROWS_MAX).then_inc(w_amax_done, 1)
            with pool.Fori(TB // 2, T // 2) as j:
                inverse_deviation(2 * j, 0)
                inverse_deviation(2 * j + 1, 1)
            old, new = slice(0, T - TB), slice(T - TB, T)
            pool.wait_ge(var1_ready, 1)
            nc.gpsimd.tensor_tensor(rstd1[:, old], var1[:, old], minus_half[:, old], ALU.pow).then_inc(rstd1_ready, 1)
            pool.wait_ge(var1_ready, 2)
            nc.gpsimd.tensor_tensor(rstd1[:, new], var1[:, new], minus_half[:, new], ALU.pow).then_inc(rstd1_ready, 1)
            pool.wait_ge(x_amax_rows, 1)
            nc.gpsimd.partition_all_reduce(small[:, 3:4], small[:, 2:3], P, ROWS_MAX).then_inc(x_amax_done, 1)

            with pool.Fori(0, T // X2) as q:
                for i in range(X2):
                    pool.wait_ge(y_ready, q * X2 + i + 1)
                    nc.gpsimd.tensor_tensor(x2[i], x2[i], y_t[i % 2], ALU.add).then_inc(sum_ready, 1)

        @block.tensor
        def _(pe):
            use = [0]

            def next_slot():
                n = use[0]
                use[0] += 1
                if n >= 4:
                    pe.wait_ge(turned_read, n - 3)
                return slots0[n % 4]

            pe.wait_ge(const_made, 6)
            pe.wait_ge(got_ctx, 16)
            to = next_slot()
            for lt in range(LT):
                for a in range(KEYS // P):
                    mm = nc.tensor.transpose(to[:, (lt * 4 + a) * P:(lt * 4 + a + 1) * P],
                                             ctx_f[:, a, lt * P:(lt + 1) * P], ident[:])
            mm.then_inc(turned, 1)
            for q in range(4):
                pe.wait_ge(got_wkv[q], 16)
                to = next_slot()
                for lt in range(LT):
                    for a in range(4):
                        mm = nc.tensor.transpose(to[:, (lt * 4 + a) * P:(lt * 4 + a + 1) * P],
                                                 wkv_f[:, 4 * q + a, lt * P:(lt + 1) * P], ident[:])
                mm.then_inc(turned, 1)
            for g2 in range(NG // 2):
                to = next_slot()
                if g2 % 4 == 0:
                    pe.wait_ge(turned_read, USES_CTX + 2 + g2 // 2)
                for half in range(2):
                    g = 2 * g2 + half
                    for lt in range(LT):
                        mm = nc.tensor.matmul(to[:, half * HALF:(half + 1) * HALF],
                                              wkv_t[:, lt, g * P:(g + 1) * P], ctx_t[:, lt, :],
                                              start=(lt == 0), stop=(lt == LT - 1))
                mm.then_inc(turned, 1)

            def make_m(ct, n):
                to, free, full = ((ps_x, x_free, x_full), (ps_p, p_free, p_full))[ct % 2]
                if not is_step(n, 0):
                    pe.wait_ge(free, n)
                for h in range(NH):
                    cols = to[:, h * SK:(h + 1) * SK]
                    w = wq_stack[:, h, ct * P:(ct + 1) * P]
                    nc.tensor.matmul(cols, w, k_hilo[:, h, :], start=True, stop=False)
                    mm = nc.tensor.matmul(cols, w, k_lohi[:, h, :], start=False, stop=True)
                mm.then_inc(full, 1)

            def make_n(j, n):
                to, free, full = ((ps_x, x_free, x_full), (ps_p, p_free, p_full))[j % 2]
                pe.wait_ge(free, n)
                for i, (vs, ws) in enumerate(PASSES):
                    for half in range(2):
                        cols = slice(half * HALF, (half + 1) * HALF)
                        mm = nc.tensor.matmul(to[:, cols], v_diag[:, vs, j, :], wo_t[:, ws, j, cols],
                                              start=(i == 0), stop=(i == len(PASSES) - 1))
                mm.then_inc(full, 1)

            def split_product(to, left, right, full, weave=None):
                for c in range(CT):
                    for i, (ls, rs) in enumerate(PASSES):
                        for half in range(2):
                            cols = slice(half * HALF, (half + 1) * HALF)
                            mm = nc.tensor.matmul(to[:, cols], left[:, ls, c * P:(c + 1) * P], right[:, rs, c, cols],
                                                  start=(c == 0 and i == 0),
                                                  stop=(c == CT - 1 and i == len(PASSES) - 1))
                    if c == CT - 1:
                        mm.then_inc(full, 1)
                    if weave is not None:
                        weave(c)

            def turn(to, tile, full, by=ident):
                for c in range(CT):
                    mm = nc.tensor.transpose(to[:, c * P:(c + 1) * P], tile[:, c * P:(c + 1) * P], by[:])
                mm.then_inc(full, 1)

            def turn_w8(a):
                pe.wait_ge(w8_ready, a + 1)
                turn(w8_ps, w8_q[a % 2], w8_full, ident_bf)

            def step(b, tt, e, t):
                known = isinstance(t, int)
                last = known and t >= T - TB
                xb, pb = x_uses(b, tt), p_uses(b, tt)
                if last and tt >= 2:
                    pe.wait_ge(w8_read, tt - 1)
                pe.wait_ge(p_ready, t + 1)
                pe.wait_ge(p_free, pb)
                turn(ps_p, pr, p_full)
                n_here = is_step(tt, 0)
                if n_here:
                    pe.wait_ge(got_v, 64 * b + 64)
                if not known or t + 1 < T:
                    pe.wait_ge(x_free, xb)
                    pe.wait_ge(s_read, t + 1)
                    split_product(ps_s, xt_buf, m_buf, s_full,
                                  (lambda c: make_n(c, (xb, pb + 1)[c % 2] + c // 2)) if n_here else None)
                if not known or t + 2 < T:
                    pe.wait_ge(xn_ready, t + 3)
                    if n_here:
                        pe.wait_ge(x_free, xb + QUAD)
                    turn(ps_x, xn[e], x_full)
                pe.wait_ge(p_free, pb + 1 + QUAD * n_here)
                if last and tt >= 1:
                    turn_w8(tt - 1)
                pe.wait_ge(x1_ready, t + 1)
                if is_step(tt, TB - 2) and not last:
                    pe.wait_ge(got_k, 128 * b + 256)
                    split_product(ps_o, pt_buf, n_buf, o_full, lambda c: make_m(c, (xb + 1, pb + 1)[c % 2] + c // 2))
                else:
                    split_product(ps_o, pt_buf, n_buf, o_full)

            pe.wait_ge(turned_read, USES0)
            pe.wait_ge(got_k, 128)
            pe.wait_ge(wq_moved, 16 * 16)
            for j in range(NP):
                make_m(j, j // 2)
                if j == 0:
                    pe.wait_ge(wout_sum, CT)
                if j >= 2:
                    pe.wait_ge(wt_free, j - 1)
                to = (ps_s, ps_o)[j % 2]
                for a in range(CT):
                    mm = nc.tensor.transpose(to[:, a * P:(a + 1) * P], wout_f[:, a, j * P:(j + 1) * P], ident[:])
                mm.then_inc(wt_full, 1)
            pe.wait_ge(x_free, QUAD)
            pe.wait_ge(xn_ready, 1)
            turn(ps_x, xn[0], x_full)
            pe.wait_ge(wt_free, NP)
            pe.wait_ge(p_free, QUAD)
            pe.wait_ge(x_free, QUAD + 1)
            split_product(ps_s, xt_buf, m_buf, s_full)
            pe.wait_ge(xn_ready, 2)
            turn(ps_x, xn[1], x_full)

            with pe.Fori(0, B - 1) as b:
                batch(pe, b, step)
            batch(pe, B - 1, step, unroll=True)
            pe.wait_ge(w8_read, CT - 1)
            turn_w8(CT - 1)

            def turn_r(t, e, first):
                pe.wait_ge(r_ready, t + 1)
                if not first:
                    pe.wait_ge(rt_ready, t - 1)
                turn(r_ps[e], r_t[e], r_full, ident_bf)

            def linear(t, e, first):
                pe.wait_ge(rt_ready, t + 1)
                if not first:
                    pe.wait_ge(y_ready, t - 1)
                for c in range(CT):
                    for half in range(2):
                        cols = slice(half * HALF, (half + 1) * HALF)
                        mm = nc.tensor.matmul(y_ps[e][:, cols], rt_t[e][:, c * P:(c + 1) * P], w8_t[:, c, cols],
                                              start=(c == 0), stop=(c == CT - 1))
                mm.then_inc(y_full, 1)

            pe.wait_ge(w8_read, CT)
            pe.wait_ge(x1_ready, T + 1)
            turn_r(0, 0, True)
            turn_r(1, 1, True)
            linear(0, 0, True)
            turn_r(2, 0, False)
            linear(1, 1, True)
            with pe.Fori(1, T // 2 - 1) as j:
                turn_r(2 * j + 1, 1, False)
                linear(2 * j, 0, False)
                turn_r(2 * j + 2, 0, False)
                linear(2 * j + 1, 1, False)
            turn_r(T - 1, 1, False)
            linear(T - 2, 0, False)
            linear(T - 1, 1, False)

        @block.scalar
        def _(act):
            def copy_out(n, to):
                act.wait_ge(turned, n + 1)
                nc.scalar.activation(to, slots0[n % 4][:].rearrange("p (a k) -> p a k", a=2), ACT.Copy).then_inc(turned_read, 1)

            copy_out(0, ctx_t)
            for q in range(4):
                copy_out(1 + q, wkv_t[:, :, q * HALF:(q + 1) * HALF])
            for g2 in range(USES_KV):
                if g2 == 6:
                    act.wait_ge(scales_made, 1)
                    for i in range(2):
                        part = slice(4 * i, 4 * i + 4)
                        nc.scalar.activation(k_hi_t[:, part, :], k_f[:, part, :], ACT.Copy,
                                             scale=to_f16[:, 1:2]).then_inc(k_hi, 1)
                kv_to = (k_f, v_f)[g2 // 4]
                copy_out(USES_CTX + USES_WKV + g2, kv_to[:, 2 * (g2 % 4):2 * (g2 % 4) + 2, :])
            act.wait_ge(k_split, 1)
            for i in range(4):
                pairs = slice(2 * i, 2 * i + 2)
                nc.scalar.activation(wq_nat_hi[:, pairs, :], wq_f[:, pairs, :], ACT.Copy,
                                     scale=to_f16[:, 0:1]).then_inc(wq_hi, 1)
            for a in range(CT):
                if a % 4 == 0:
                    act.wait_ge(got_wout[a // 4], 16)
                if a > 0:
                    act.wait_ge(wout_sum, a)
                nc.scalar.activation(ps_o[:], wout_f[:, a, :], ACT.Abs, accum_out=wout_sums[:, a:a + 1]).then_inc(wout_sum, 1)

            def take_hi(to, slot, full, n, scale, done):
                act.wait_ge(full, n)
                nc.scalar.activation(to, slot[:], ACT.Copy, scale=scale).then_inc(done, 1)

            def take_mn(to, c, n, scale):
                slot, full, done = ((ps_x, x_full, x_hi), (ps_p, p_full, p_hi))[c % 2]
                take_hi(to[:, 0, c, :], slot, full, n + 1, scale, done)

            def exponentials(t):
                act.wait_ge(s_read, t + 1)
                nc.scalar.activation(ex, sub, ACT.Exp, scale=score_scale[:]).then_inc(exp_done, 1)

            def deviations(t, e):
                act.wait_ge(mean_ready, t + 1)
                nc.scalar.activation(dev, x1[e], ACT.Abs, bias=neg_mean[e][:]).then_inc(dev_ready, 1)

            def quotients(a):
                if a == 0:
                    act.wait_ge(w_scale_made, 1)
                else:
                    act.wait_ge(w8_ready, a)
                nc.scalar.activation(w_tmp[0], w8_raw[:, a, :], ACT.Copy, scale=small[:, 5:6]).then_inc(w_quot, 1)

            def copy_w8(a):
                act.wait_ge(w8_full, a + 1)
                nc.scalar.activation(w8_t[:, :, a * P:(a + 1) * P], w8_ps.rearrange("p (c o) -> p c o", c=CT),
                                     ACT.Copy).then_inc(w8_read, 1)

            def step(b, tt, e, t):
                known = isinstance(t, int)
                last = known and t >= T - TB
                xb, pb = x_uses(b, tt), p_uses(b, tt)
                take_hi(pt_buf[:, 0, :], ps_p, p_full, pb + 1, P_SCALE, p_hi)
                grown = 0
                grow_n = lambda c: take_mn(n_buf, c, (xb, pb + 1)[c % 2] + c // 2, N_SCALE)
                if is_step(tt, 0):
                    grown = QUAD
                    if known and t == 0:
                        act.wait_ge(kv_stored, 64)
                    grow_n(0)
                    grow_n(1)
                if not (known and t == 0):
                    deviations(t - 1, 1 - e)
                if last:
                    quotients(tt)
                if is_step(tt, 0):
                    for c in range(2, CT):
                        grow_n(c)
                if not known or t + 2 < T:
                    take_hi(xt_buf[:, 0, :], ps_x, x_full, xb + grown + 1, XN_SCALE, x_hi)
                if last and tt >= 1:
                    copy_w8(tt - 1)
                if not known or t + 1 < T:
                    exponentials(t + 1)
                if is_step(tt, TB - 2) and not last:
                    for c in range(CT):
                        take_mn(m_buf, c, (xb + 1, pb + 1)[c % 2] + c // 2, M_SCALE)

            def take_wout(j):
                act.wait_ge(wt_full, j + 1)
                nc.scalar.activation(wo_t[:, 0, j, :], (ps_s, ps_o)[j % 2][:], ACT.Copy, scale=to_f16[:, 2:3]).then_inc(wt_hi, 1)

            act.wait_ge(wq_moved, 16 * 16)
            take_mn(m_buf, 0, 0, M_SCALE)
            take_mn(m_buf, 1, 0, M_SCALE)
            act.wait_ge(scales_made, 2)
            for j in range(NP):
                take_wout(j)
                if j + 2 < NP:
                    take_mn(m_buf, j + 2, (j + 2) // 2, M_SCALE)
            act.wait_ge(kv_stored, 32)
            take_hi(xt_buf[:, 0, :], ps_x, x_full, QUAD + 1, XN_SCALE, x_hi)
            nc.scalar.activation(v_hi_t, v_f, ACT.Copy, scale=to_f16[:, 3:4]).then_inc(v_hi, 1)
            take_hi(xt_buf[:, 0, :], ps_x, x_full, QUAD + 2, XN_SCALE, x_hi)
            exponentials(0)
            batch(act, 0, step)
            with act.Fori(1, B - 1) as b:
                batch(act, b, step)
            batch(act, B - 1, step, unroll=True)
            copy_w8(CT - 1)
            deviations(T - 1, 1)

            def values(t, i, e, first):
                act.wait_ge(got_x1[i], (t - i) * (16 // X2) + 16)
                if not first:
                    act.wait_ge(g_done, t - 1)
                nc.scalar.activation(u_t[e], x2[i], ACT.Identity, bias=quant_b20[:, bass.ds(t, 1)],
                                     scale=quant_a20[:, bass.ds(t, 1)]).then_inc(u_ready, 1)
                if e == 0:
                    if not first:
                        act.wait_ge(a_done, t - 1)
                    nc.scalar.activation(v_t[e], x2[i], ACT.Identity, bias=quant_b[:, bass.ds(t, 1)],
                                         scale=quant_a[:, bass.ds(t, 1)]).then_inc(v_ready, 1)

            def copy_rt(t, e, first):
                act.wait_ge(r_full, t + 1)
                if not first:
                    act.wait_ge(y_full, t - 1)
                nc.scalar.activation(rt_t[e], r_ps[e], ACT.Copy).then_inc(rt_ready, 1)

            def scaled(t, e, first):
                act.wait_ge(y_full, t + 1)
                if not first:
                    act.wait_ge(sum_ready, t - 1)
                nc.scalar.activation(y_t[e], y_ps[e][:], ACT.Copy, scale=small[:, 8:9]).then_inc(y_ready, 1)

            act.wait_ge(quant_ready, 1)
            values(0, 0, 0, True)
            values(1, 1, 1, True)
            copy_rt(0, 0, True)
            values(2, 2, 0, False)
            copy_rt(1, 1, True)
            values(3, 3, 1, False)
            scaled(0, 0, True)
            copy_rt(2, 0, False)
            values(4, 4, 0, False)
            scaled(1, 1, True)
            copy_rt(3, 1, False)
            values(5, 5, 1, False)

            def step2(t, i):
                scaled(t, i % 2, False)
                copy_rt(t + 2, i % 2, False)
                values(t + 4, (i + 4) % X2, i % 2, False)

            for t in range(2, 4):
                step2(t, t)
            with act.Fori(0, T // X2 - 1) as q:
                for i in range(X2):
                    step2(q * X2 + 4 + i, (4 + i) % X2)
            for t in range(T - 4, T):
                scaled(t, t % 2, False)
                if t + 2 < T:
                    copy_rt(t + 2, t % 2, False)

        @block.vector
        def _(dve):
            steps = [0]

            def then(ins):
                steps[0] += 1
                ins.then_inc(dve_step, 1)
                dve.wait_ge(dve_step, steps[0])

            for i in range(2):
                dve.wait_ge(got_wq[i], 16)
                nc.vector.tensor_reduce(small[:, 4 + i:5 + i], wq_f[:, 4 * i:4 * i + 4, :], AX.XY, ALU.max,
                                        apply_absolute_value=True).then_inc(dve_step, 1)
            dve.wait_ge(turned_read, USES_CTX + USES_WKV + 4)
            nc.vector.tensor_reduce(amax4[:, 1:2], k_f, AX.XY, ALU.max, apply_absolute_value=True).then_inc(dve_step, 1)
            steps[0] = 3
            dve.wait_ge(dve_step, steps[0])
            nc.vector.tensor_tensor(amax4[:, 0:1], small[:, 4:5], small[:, 5:6], ALU.max).then_inc(amax_rows, 1)

            def powers(cols, done):
                dve.wait_ge(amax_done, done)
                then(nc.vector.tensor_scalar(amax4_all[:, cols], amax4_all[:, cols], AMAX_FLOOR, None, ALU.max))
                then(nc.vector.tensor_scalar(amax4_all[:, cols].bitcast(U32), amax4_all[:, cols].bitcast(U32),
                                             EXPONENT_BITS, None, ALU.bitwise_and))
                then(nc.vector.tensor_scalar(from_f16[:, cols], amax4_all[:, cols], 1.0 / AMAX_TO, None, ALU.mult))
                then(nc.vector.reciprocal(to_f16[:, cols], from_f16[:, cols]))

            powers(slice(0, 2), 1)
            nc.vector.tensor_scalar(score_scale[:], from_f16[:, 0:1], from_f16[:, 1:2],
                                    1.0 / (M_SCALE * XN_SCALE * HD ** 0.5), ALU.mult, ALU.mult).then_inc(scales_made, 1)
            for i in range(2):
                part = slice(4 * i, 4 * i + 4)
                dve.wait_ge(k_hi, i + 1)
                lo = nc.vector.scalar_tensor_tensor(out=k_lo_t[:, part, :], in0=k_f[:, part, :], scalar=to_f16[:, 1:2],
                                                    in1=k_hi_t[:, part, :], op0=ALU.mult, op1=ALU.subtract)
                lo.then_inc((dve_step, k_split)[i], 1)
            steps[0] += 1
            dve.wait_ge(turned_read, USES0)
            for i in range(4):
                pairs = slice(2 * i, 2 * i + 2)
                dve.wait_ge(wq_hi, i + 1)
                nc.vector.scalar_tensor_tensor(out=wq_nat_lo[:, pairs, :], in0=wq_f[:, pairs, :], scalar=to_f16[:, 0:1],
                                               in1=wq_nat_hi[:, pairs, :], op0=ALU.mult,
                                               op1=ALU.subtract).then_inc(wq_split, 1)
            then(nc.vector.tensor_reduce(amax4[:, 3:4], v_f, AX.XY, ALU.max, apply_absolute_value=True))

            def take_lo(to, hi, slot, n, scale, hi_done, free):
                dve.wait_ge(hi_done, n)
                nc.vector.scalar_tensor_tensor(out=to, in0=slot[:], scalar=scale, in1=hi, op0=ALU.mult,
                                               op1=ALU.subtract).then_inc(free, 1)

            def take_mn(to, c, n, scale):
                slot, done, free = ((ps_x, x_hi, x_free), (ps_p, p_hi, p_free))[c % 2]
                take_lo(to[:, 1, c, :], to[:, 0, c, :], slot, n + 1, scale, done, free)

            def variance(t, e):
                dve.wait_ge(got_xa[e], (t - e) * 8 + 16)
                for half in range(2):
                    nc.vector.bn_stats(stats_a[:, half, :], xa[e][:, half * HALF:(half + 1) * HALF]).then_inc(a_stats, 1)
                dve.wait_ge(a_stats, 2 * t + 2)
                nc.vector.memset(wait_carrier[:], 0.0)
                nc.vector.bn_aggr(mv_a[e][:], stats_a[:].rearrange("p a b -> p (a b)")).then_inc(a_aggr, 1)
                dve.wait_ge(a_aggr, t + 1)
                nc.vector.tensor_scalar(veps[e][:], mv_a[e][:, 1:2], LN_EPS, None, ALU.add).then_inc(var_ready, 1)

            def normalise(t, e):
                dve.wait_ge(rstd_ready, t + 1)
                nc.vector.tensor_scalar(xn[e], xa[e], mv_a[e][:, 0:1], rstd[e][:], ALU.subtract,
                                        ALU.mult).then_inc(xn_ready, 1)

            def heads(ap):
                return ap.rearrange("p (h k) -> p h k", h=NH)

            def across(ap):
                return ap.unsqueeze(2).to_broadcast([P, NH, SK])

            def mask_scores(t):
                dve.wait_ge(s_full, t + 1)
                nc.vector.tensor_tensor(heads(ps_s[:]), heads(ps_s[:]),
                                        causal[:].unsqueeze(1).to_broadcast([P, NH, SK]), ALU.add).then_inc(masked, 1)

            def maxima(t, masks=None):
                if masks is None:
                    dve.wait_ge(s_full, t + 1)
                else:
                    dve.wait_ge(masked, masks)
                nc.vector.tensor_reduce(hmax[:], heads(ps_s[:]), AX.X, ALU.max).then_inc(max_done, 1)
                dve.wait_ge(max_done, t + 1)
                nc.vector.tensor_tensor(heads(sub), heads(ps_s[:]), across(hmax[:]), ALU.subtract).then_inc(s_read, 1)

            def probabilities(t):
                dve.wait_ge(exp_done, t + 1)
                nc.vector.tensor_reduce(hsum[:], heads(ex), AX.X, ALU.add).then_inc(sum_done, 1)
                dve.wait_ge(sum_done, t + 1)
                nc.vector.reciprocal(hinv[:], hsum[:]).then_inc(inv_done, 1)
                dve.wait_ge(inv_done, t + 1)
                nc.vector.tensor_tensor(heads(pr), heads(ex), across(hinv[:]), ALU.mult).then_inc(p_ready, 1)

            def residual(t, e, stored=True):
                dve.wait_ge(o_full, t + 1)
                dve.wait_ge(got_xr[e], (t - e) * 8 + 16)
                if stored:
                    dve.wait_ge(x1_stored[e], (t - e) * 8)
                nc.vector.scalar_tensor_tensor(out=x1[e], in0=ps_o[:], scalar=out_scale[:], in1=xr[e], op0=ALU.mult,
                                               op1=ALU.add).then_inc(x1_ready, 1)
                dve.wait_ge(x1_ready, t + 2)
                for half in range(2):
                    nc.vector.bn_stats(stats_b[:, half, :], x1[e][:, half * HALF:(half + 1) * HALF]).then_inc(b_stats, 1)
                dve.wait_ge(b_stats, 2 * t + 2)
                nc.vector.memset(wait_carrier[:], 0.0)
                nc.vector.bn_aggr(mv_b[:], stats_b[:].rearrange("p a b -> p (a b)")).then_inc(b_aggr, 1)
                dve.wait_ge(b_aggr, t + 1)
                nc.vector.tensor_scalar(neg_mean[e][:], mv_b[:, 0:1], -1.0, None, ALU.mult).then_inc(mean_ready, 1)
                nc.vector.tensor_copy(mean1[:, bass.ds(t, 1)], mv_b[:, 0:1]).then_inc(kept, 1)
                nc.vector.tensor_scalar(var1[:, bass.ds(t, 1)], mv_b[:, 1:2], LN_EPS, None, ALU.add).then_inc(kept, 1)

            def peak(t):
                dve.wait_ge(dev_ready, t + 1)
                nc.vector.tensor_reduce(peak1[:, bass.ds(t, 1)], dev, AX.X, ALU.max).then_inc(x1_done, 1)

            def round_e4m3(rounded, v, u, g, s):
                then(nc.vector.tensor_scalar(g.bitcast(U32), u.bitcast(U32), EXPONENT_BITS, HALF_BIT,
                                             ALU.bitwise_and, ALU.bitwise_or))
                then(nc.vector.scalar_tensor_tensor(out=s, in0=g, scalar=ROUND_LEAST, in1=v, op0=ALU.max, op1=ALU.add))
                return nc.vector.scalar_tensor_tensor(out=rounded, in0=g, scalar=ROUND_LEAST, in1=s, op0=ALU.max,
                                                      op1=ALU.subtract)

            def quantise_w8(a):
                SPLIT16 = 2.0 ** 8 + 1.0
                w, s, v, u = w_tmp
                dve.wait_ge(w_quot, a + 1)
                then(nc.vector.scalar_tensor_tensor(out=s, in0=w, scalar=SPLIT16, in1=w, op0=ALU.mult, op1=ALU.subtract))
                then(nc.vector.scalar_tensor_tensor(out=v, in0=w, scalar=SPLIT16, in1=s, op0=ALU.mult, op1=ALU.subtract))
                then(nc.vector.tensor_scalar(u, v, ROUND_SHIFT, None, ALU.mult))
                if a >= 2:
                    dve.wait_ge(w8_full, a - 1)
                round_e4m3(w8_q[a % 2], v, u, w, s).then_inc(w8_ready, 1)
                dve.wait_ge(w8_ready, a + 1)

            def step(b, tt, e, t):
                known = isinstance(t, int)
                last = known and t >= T - TB
                xb, pb = x_uses(b, tt), p_uses(b, tt)
                take_lo(pt_buf[:, 1, :], pt_buf[:, 0, :], ps_p, pb + 1, P_SCALE, p_hi, p_free)
                norm = not known or t + 3 < T
                grown = 0
                grow_n = lambda c: take_mn(n_buf, c, (xb, pb + 1)[c % 2] + c // 2, N_SCALE)
                grow_m = lambda c: take_mn(m_buf, c, (xb + 1, pb + 1)[c % 2] + c // 2, M_SCALE)
                if is_step(tt, 0):
                    grown = QUAD
                    grow_n(0)
                if not (known and t == 0):
                    residual(t - 1, 1 - e, stored=not (known and t < 3))
                if is_step(tt, 0):
                    grow_n(1)
                if norm:
                    variance(t + 3, 1 - e)
                if is_step(tt, 0):
                    grow_n(2)
                if not (known and t == 0):
                    peak(t - 1)
                if norm:
                    normalise(t + 3, 1 - e)
                if is_step(tt, 0):
                    for c in range(3, CT):
                        grow_n(c)
                if not known or t + 1 < T:
                    if is_step(tt, TB - 1):
                        mask_scores(t + 1)
                        maxima(t + 1, masks=b + 2)
                    else:
                        maxima(t + 1)
                if not known or t + 2 < T:
                    take_lo(xt_buf[:, 1, :], xt_buf[:, 0, :], ps_x, xb + grown + 1, XN_SCALE, x_hi, x_free)
                grow = is_step(tt, TB - 2) and not last
                if grow:
                    grow_m(0)
                if not known or t + 1 < T:
                    probabilities(t + 1)
                if grow:
                    for c in range(1, CT):
                        grow_m(c)
                if known and t == 3:
                    dve.wait_ge(got_w8, 16)
                    nc.vector.tensor_reduce(small[:, 0:1], w8_raw[:], AX.XY, ALU.max,
                                            apply_absolute_value=True).then_inc(w_amax_rows, 1)
                if known and t == 6:
                    dve.wait_ge(w_amax_done, 1)
                    then(nc.vector.tensor_scalar(small[:, 4:5], small[:, 1:2], 1.0 / E4M3_MAX, 1e-12, ALU.mult, ALU.max))
                    nc.vector.reciprocal(small[:, 5:6], small[:, 4:5]).then_inc(w_scale_made, 1)
                if last:
                    if tt == 1:
                        dve.wait_ge(kept, 2 * (T - TB))
                        nc.vector.tensor_copy(small[:, 15:16], mv_b[:, 0:1]).then_inc(var1_ready, 1)
                    quantise_w8(tt)

            def take_wout(j):
                dve.wait_ge(wt_hi, j + 1)
                nc.vector.scalar_tensor_tensor(out=wo_t[:, 1, j, :], in0=(ps_s, ps_o)[j % 2][:], scalar=to_f16[:, 2:3],
                                               in1=wo_t[:, 0, j, :], op0=ALU.mult, op1=ALU.subtract).then_inc(wt_free, 1)

            variance(0, 0)
            variance(1, 1)
            dve.wait_ge(wq_moved, 16 * 16)
            normalise(0, 0)
            normalise(1, 1)
            take_mn(m_buf, 0, 0, M_SCALE)
            dve.wait_ge(wout_sum, CT)
            nc.vector.tensor_reduce(amax4[:, 2:3], wout_sums[:], AX.X, ALU.add).then_inc(amax_rows, 1)
            take_mn(m_buf, 1, 0, M_SCALE)
            powers(slice(2, 4), 2)
            nc.vector.tensor_scalar(out_scale[:], from_f16[:, 2:3], from_f16[:, 3:4],
                                    1.0 / (N_SCALE * P_SCALE), ALU.mult, ALU.mult).then_inc(scales_made, 1)
            for j in range(NP):
                take_wout(j)
                if j + 2 < NP:
                    take_mn(m_buf, j + 2, (j + 2) // 2, M_SCALE)
            take_lo(xt_buf[:, 1, :], xt_buf[:, 0, :], ps_x, QUAD + 1, XN_SCALE, x_hi, x_free)
            dve.wait_ge(v_hi, 1)
            nc.vector.scalar_tensor_tensor(out=v_lo_t, in0=v_f, scalar=to_f16[:, 3:4], in1=v_hi_t, op0=ALU.mult,
                                           op1=ALU.subtract).then_inc(v_split, 1)
            variance(2, 0)
            mask_scores(0)
            maxima(0, masks=1)
            take_lo(xt_buf[:, 1, :], xt_buf[:, 0, :], ps_x, QUAD + 2, XN_SCALE, x_hi, x_free)
            normalise(2, 0)
            probabilities(0)
            nc.vector.memset(wait_carrier[:], 0.0).then_inc(x1_ready, 1)
            batch(dve, 0, step, unroll=True)
            with dve.Fori(1, B - 1) as b:
                batch(dve, b, step)
            batch(dve, B - 1, step, unroll=True)
            residual(T - 1, 1)
            dve.wait_ge(kept, 2 * T)
            nc.vector.tensor_copy(small[:, 15:16], mv_b[:, 0:1]).then_inc(var1_ready, 1)
            peak(T - 1)

            dve.wait_ge(rstd1_ready, 2)
            dve.wait_ge(x1_done, T)
            then(nc.vector.tensor_tensor(quant_a20, peak1[:], rstd1[:], ALU.mult))
            nc.vector.tensor_reduce(small[:, 2:3], quant_a20, AX.X, ALU.max).then_inc(x_amax_rows, 1)
            dve.wait_ge(x_amax_done, 1)
            then(nc.vector.tensor_scalar(small[:, 6:7], small[:, 3:4], 1.0 / E4M3_MAX, 1e-12, ALU.mult, ALU.max))
            then(nc.vector.reciprocal(small[:, 7:8], small[:, 6:7]))
            then(nc.vector.tensor_scalar(quant_a[:], rstd1[:], small[:, 7:8], None, ALU.mult))
            then(nc.vector.scalar_tensor_tensor(out=quant_b[:], in0=mean1[:], scalar=-1.0, in1=quant_a[:], op0=ALU.mult,
                                                op1=ALU.mult))
            nc.vector.tensor_scalar(small[:, 8:9], small[:, 6:7], small[:, 4:5], None, ALU.mult).then_inc(dve_step, 1)
            nc.vector.tensor_scalar(quant_a20, quant_a[:], ROUND_SHIFT, None, ALU.mult).then_inc(dve_step, 1)
            steps[0] += 2
            dve.wait_ge(dve_step, steps[0])
            nc.vector.tensor_scalar(quant_b20, quant_b[:], ROUND_SHIFT, None, ALU.mult).then_inc(quant_ready, 1)

            def constant_g(t, e, first=False):
                dve.wait_ge(u_ready, t + 1)
                if not first:
                    dve.wait_ge(r_ready, t - 1)
                nc.vector.tensor_scalar(g_t[e].bitcast(U32), u_t[e].bitcast(U32), EXPONENT_BITS, HALF_BIT,
                                        ALU.bitwise_and, ALU.bitwise_or).then_inc(g_done, 1)

            def value_v(t, i, first=False):
                dve.wait_ge(got_x1[i], (t - i) * (16 // X2) + 16)
                if not first:
                    dve.wait_ge(a_done, t - 1)
                nc.vector.tensor_scalar(v_t[1], x2[i], quant_a[:, bass.ds(t, 1)], quant_b[:, bass.ds(t, 1)], ALU.mult,
                                        ALU.add).then_inc(v_odd, 1)

            def rounded(t, e, first=False):
                dve.wait_ge(a_done, t + 1)
                if not first:
                    dve.wait_ge(r_full, t - 1)
                nc.vector.scalar_tensor_tensor(out=r_t[e], in0=g_t[e], scalar=ROUND_LEAST, in1=a_t[e], op0=ALU.max,
                                               op1=ALU.subtract).then_inc(r_ready, 1)

            def two_tiles(base, i, before, last=False):
                t, pairs = base + i, before + i // 2 + 1
                first = isinstance(t, int) and t == 0
                dve.wait_ge(g_done, t + 1)
                dve.wait_ge(v_ready, pairs)
                nc.vector.scalar_tensor_tensor(out=a_t[0], in0=g_t[0], scalar=ROUND_LEAST, in1=v_t[0], op0=ALU.max,
                                               op1=ALU.add).then_inc(a_done, 1)
                value_v(t + 1, i + 1, first)
                constant_g(t + 1, 1, first)
                rounded(t, 0, first)
                dve.wait_ge(g_done, t + 2)
                dve.wait_ge(v_odd, pairs)
                nc.vector.scalar_tensor_tensor(out=a_t[1], in0=g_t[1], scalar=ROUND_LEAST, in1=v_t[1], op0=ALU.max,
                                               op1=ALU.add).then_inc(a_done, 1)
                if not last:
                    constant_g(t + 2, 0)
                rounded(t + 1, 1, first)

            constant_g(0, 0, True)
            for i in range(0, X2, 2):
                two_tiles(0, i, 0)
            with dve.Fori(1, T // X2 - 1) as q:
                for i in range(0, X2, 2):
                    two_tiles(q * X2, i, q * (X2 // 2))
            for i in range(0, X2, 2):
                two_tiles(T - X2, i, (T - X2) // 2, last=(i == X2 - 2))


_INS = ['x', 'ctx_512', 'L0_xattn_Wq', 'L0_xattn_Wkv_expand', 'L0_xattn_Wout', 'L0_ffn_weight']
_OUTS = [((8, 1024, 1024), 'float32')]


def kernel(**inputs):
    import numpy as _np
    import concourse.bacc as _bacc
    from concourse import mybir as _mybir
    from concourse.bass_utils import run_bass_kernel_spmd as _run

    nc = _bacc.Bacc("TRN2", target_bir_lowering=False, num_devices=1)
    arrays, args = {}, []
    for name in _INS:
        a = _np.ascontiguousarray(inputs[name])
        arrays[f"in_{name}_dram"] = a
        args.append(nc.dram_tensor(f"in_{name}_dram", a.shape, _mybir.dt.from_np(a.dtype), kind="ExternalInput").ap())
    for i, (shape, dtype) in enumerate(_OUTS):
        dt = _mybir.dt.from_np(_np.dtype(dtype))
        args.append(nc.dram_tensor(f"out_{i}_dram", shape, dt, kind="ExternalOutput").ap())
    xattn_ffn_kernel(nc, *args)
    r = _run(nc, [arrays], core_ids=[0])
    return r.results[0]["out_0_dram"]
```

```python
from contextlib import ExitStack

import concourse.bass as bass
from concourse import mybir

F32 = mybir.dt.float32
F16 = mybir.dt.float16
BF16 = mybir.dt.bfloat16
U32 = mybir.dt.uint32
ALU = mybir.AluOpType
ACT = mybir.ActivationFunctionType
AX = mybir.AxisListType
ROWS_MAX = bass.bass_isa.ReduceOp.max

P = 128
HD = 64
LN_EPS = 1e-5
E4M3_MAX = 448.0

AMAX_TO = 2.0 ** 13
M_SCALE = 2.0 ** -20
N_SCALE = 2.0 ** -14
XN_SCALE = 2.0 ** 10
P_SCALE = 2.0 ** 14
AMAX_FLOOR = 2.0 ** -40
ROUND_SHIFT = 2.0 ** 20
ROUND_LEAST = 1.5 * 2.0 ** 14
EXPONENT_BITS = 0x7F800000
HALF_BIT = 0x00400000
MASKED = -3.0e38


def xattn_ffn_kernel(nc, x, ctx, Wq, Wkv, Wout, Wffn, out):
    B, S, H = x.shape
    SK, L = ctx.shape[1:]
    NH = H // HD
    NP = NH // 2
    CT = H // P
    LT = L // P
    TB = S // P
    T = B * TB
    KEYS = B * SK
    HALF = 512
    assert SK == HD and NP == CT and KEYS == HALF and TB == 8

    x_rows = x.rearrange("b s h -> (b s) h")
    out_rows = out.rearrange("b s h -> (b s) h")

    with ExitStack() as scope:
        def sb(name, shape, dt):
            return scope.enter_context(nc.sbuf_tensor(name, shape, dt))

        def sem(name):
            return scope.enter_context(nc.semaphore(name))

        x1_dram = nc.dram_tensor("x1_scratch", [T * P, H], F32, kind="Internal").ap()
        kv_dram = nc.dram_tensor("kv_scratch", [2, P, 2 * NP, KEYS], F16, kind="Internal").ap()

        wq_stack = sb("wq_stack", [P, NH, H], F16)
        wo_t = sb("wo_t", [P, 2, NP, H], F16)
        m_buf = sb("m_buf", [P, 2, CT, H], F16)
        n_buf = sb("n_buf", [P, 2, NP, H], F16)
        k_hilo = sb("k_hilo", [P, NH, SK], F16)
        k_lohi = sb("k_lohi", [P, NH, SK], F16)
        v_diag = sb("v_diag", [P, 2, NP, P], F16)

        w8_raw = sb("w8_raw", [P, CT, H], BF16)

        tile_space = sb("tile_space", [P, 13, H], F32)
        xa = [tile_space[:, i, :] for i in (0, 1)]
        xr = [tile_space[:, i, :] for i in (2, 3)]
        xn = [tile_space[:, i, :] for i in (4, 5)]
        x1 = [tile_space[:, i, :] for i in (6, 7)]
        sub = tile_space[:, 8, :]
        ex = tile_space[:, 9, :]
        dev = ex
        pr = tile_space[:, 10, :]
        xt_buf = tile_space[:, 11, :].bitcast(F16).rearrange("p (s n) -> p s n", s=2)
        pt_buf = tile_space[:, 12, :].bitcast(F16).rearrange("p (s n) -> p s n", s=2)

        ident = sb("ident", [P, P], F32)
        ident_bf = sb("ident_bf", [P, P], BF16)
        causal = sb("causal", [P, SK], F32)
        minus_half = sb("minus_half", [P, T], F32)
        amax4 = sb("amax4", [P, 4], F32)
        wout_sums = sb("wout_sums", [P, CT], F32)
        amax4_all = sb("amax4_all", [P, 4], F32)
        to_f16 = sb("to_f16", [P, 4], F32)
        from_f16 = sb("from_f16", [P, 4], F32)
        score_scale = sb("score_scale", [P, 1], F32)
        out_scale = sb("out_scale", [P, 1], F32)
        small = sb("small", [P, 16], F32)
        stats_a = sb("stats_a", [P, 2, 6], F32)
        stats_b = sb("stats_b", [P, 2, 6], F32)
        mv_a = [sb(f"mv_a{i}", [P, 2], F32) for i in (0, 1)]
        mv_b = sb("mv_b", [P, 2], F32)
        veps = [sb(f"veps_x{i}", [P, 1], F32) for i in (0, 1)]
        rstd = [sb(f"rstd_x{i}", [P, 1], F32) for i in (0, 1)]
        neg_mean = [sb(f"neg_mean{i}", [P, 1], F32) for i in (0, 1)]
        wait_carrier = sb("wait_carrier", [P, 1], F32)
        hmax = sb("hmax", [P, NH], F32)
        hsum = sb("hsum", [P, NH], F32)
        hinv = sb("hinv", [P, NH], F32)
        mean1 = sb("mean1", [P, T], F32)
        var1 = sb("var1", [P, T], F32)
        rstd1 = sb("rstd1", [P, T], F32)
        peak1 = sb("peak1", [P, T], F32)
        quant_a = sb("quant_a", [P, T], F32)
        quant_b = sb("quant_b", [P, T], F32)
        quant_a20, quant_b20 = ident[:, 0:T], ident[:, T:2 * T]

        ps_s = scope.enter_context(nc.psum_tensor("ps_s", [P, H], F32))
        ps_o = scope.enter_context(nc.psum_tensor("ps_o", [P, H], F32))
        ps_x = scope.enter_context(nc.psum_tensor("ps_x", [P, H], F32))
        ps_p = scope.enter_context(nc.psum_tensor("ps_p", [P, H], F32))

        def flat(t):
            return t[:].rearrange("p a b c -> p (a b c)")

        wq_f = flat(m_buf).bitcast(F32).rearrange("p (j c) -> p j c", c=H)
        wout_f = flat(n_buf).bitcast(F32).rearrange("p (a c) -> p a c", c=H)
        wkv_f = tile_space[:, 8:12, :].rearrange("p a (b l) -> p (a b) l", l=L)
        ctx_f = tile_space[:, 12, :].rearrange("p (a l) -> p a l", l=L)
        wkv_t = tile_space[:, 4:8, :].rearrange("p (a q) r -> p a (q r)", a=LT)
        ctx_t = tile_space[:, 3, :].rearrange("p (a k) -> p a k", a=LT)
        k_f = wo_t[:, 1].rearrange("p j c -> p (j c)").bitcast(F32).rearrange("p (j k) -> p j k", k=KEYS)
        v_f = w8_raw[:].rearrange("p j c -> p (j c)").bitcast(F32).rearrange("p (j k) -> p j k", k=KEYS)
        k_hi_t, k_lo_t = (tile_space[:, i:i + 2, :].rearrange("p a c -> p (a c)").bitcast(F16)
                          .rearrange("p (j k) -> p j k", k=KEYS) for i in (8, 10))
        v_hi_t, v_lo_t = (flat(n_buf)[:, i:i + 4096].rearrange("p (j k) -> p j k", k=KEYS) for i in (0, 4096))
        wq_nat_hi = wo_t[:, 0]
        wq_nat_lo = [tile_space[:, i, :].bitcast(F16).rearrange("p (j c) -> p j c", c=H)
                     for i in (12, 0, 1, 2)]
        NG = 2 * NP
        EVEN, ODD = slice(0, HD), slice(HD, P)

        def wq_heads(e):
            return wq_stack[:].rearrange("p (j e) c -> p e j c", e=2)[:, e]

        const_made = sem("const_made")
        diag_zeroed = sem("diag_zeroed")
        got_ctx = sem("got_ctx")
        got_wkv = [sem(f"got_wkv{q}") for q in range(4)]
        got_wq = [sem(f"got_wq{i}") for i in range(4)]
        got_wout = [sem(f"got_wout{i}") for i in range(2)]
        turned = sem("turned")
        turned_read = sem("turned_read")
        wt_full = sem("wt_full")
        wt_hi = sem("wt_hi")
        wt_free = sem("wt_free")
        wout_sum = sem("wout_sum")
        amax_rows = sem("amax_rows")
        amax_done = sem("amax_done")
        scales_made = sem("scales_made")
        dve_step = sem("dve_step")
        k_hi = sem("k_hi")
        v_hi = sem("v_hi")
        wq_hi = sem("wq_hi")
        k_split = sem("k_split")
        v_split = sem("v_split")
        wq_split = sem("wq_split")
        wq_moved = [sem(f"wq_moved{i}") for i in range(4)]
        kv_stored = sem("kv_stored")
        got_k = sem("got_k")
        got_v = sem("got_v")
        got_xa = [sem("got_xa0"), sem("got_xa1")]
        got_xr = [sem("got_xr0"), sem("got_xr1")]
        var_ready = sem("var_ready")
        rstd_ready = sem("rstd_ready")
        xn_ready = sem("xn_ready")
        x_full = sem("x_full")
        x_hi = sem("x_hi")
        x_free = sem("x_free")
        p_full = sem("p_full")
        p_hi = sem("p_hi")
        p_free = sem("p_free")
        s_full = sem("s_full")
        s_read = sem("s_read")
        exp_done = sem("exp_done")
        p_ready = sem("p_ready")
        o_full = sem("o_full")
        x1_ready = sem("x1_ready")
        a_stats = sem("a_stats")
        a_aggr = sem("a_aggr")
        b_stats = sem("b_stats")
        b_aggr = sem("b_aggr")
        masked = sem("masked")
        max_done = sem("max_done")
        sum_done = sem("sum_done")
        inv_done = sem("inv_done")
        kept = sem("kept")
        mean_ready = sem("mean_ready")
        dev_ready = sem("dev_ready")
        x1_done = sem("x1_done")
        x1_stored = [sem("x1_stored0"), sem("x1_stored1")]
        var1_ready = sem("var1_ready")
        rstd1_ready = sem("rstd1_ready")
        got_w8 = sem("got_w8")
        w_amax_rows = sem("w_amax_rows")
        w_amax_done = sem("w_amax_done")
        w_scale_made = sem("w_scale_made")
        w_quot = sem("w_quot")
        x_amax_rows = sem("x_amax_rows")
        x_amax_done = sem("x_amax_done")
        w8_ready = sem("w8_ready")
        w8_full = sem("w8_full")
        w8_read = sem("w8_read")
        quant_ready = sem("quant_ready")
        g_done = sem("g_done")
        a_done = sem("a_done")
        got_x1 = [sem(f"got_x1_{i}") for i in range(8)]
        u_ready = sem("u_ready")
        v_ready = sem("v_ready")
        v_odd = sem("v_odd")
        r_ready = sem("r_ready")
        r_full = sem("r_full")
        rt_ready = sem("rt_ready")
        y_full = sem("y_full")
        y_ready = sem("y_ready")
        sum_ready = sem("sum_ready")
        out_stored = [sem(f"out_stored{i}") for i in range(8)]

        wq_flat = wq_stack[:].rearrange("p h c -> p (h c)")
        w_tmp = [wq_flat[:, i * 2048:(i + 1) * 2048].bitcast(F32) for i in range(4)]
        w8_q = [wq_flat[:, 8192 + i * H:8192 + (i + 1) * H].bitcast(BF16) for i in range(2)]
        w8_t = wo_t[:, 0].bitcast(BF16)
        w8_ps = [ps_p[:, 0:HALF].bitcast(BF16)] * (CT - 2) + [ps_s[:, 0:HALF].bitcast(BF16)] * 2
        X2 = 8
        x2 = [tile_space[:, i, :] for i in range(X2)]
        flat_n = flat(n_buf)
        v_t, u_t, g_t, a_t = ([flat_n[:, i * 2048:(i + 1) * 2048].bitcast(F32) for i in (k, k + 1)] for k in (0, 2, 4, 6))
        r_t = [tile_space[:, 10, :].bitcast(BF16)[:, i * H:(i + 1) * H] for i in (0, 1)]
        rt_t = [tile_space[:, 11, :].bitcast(BF16)[:, i * H:(i + 1) * H] for i in (0, 1)]
        y_t = [tile_space[:, 12, :].bitcast(BF16)[:, i * H:(i + 1) * H] for i in (0, 1)]
        r_ps = [ps_x[:, 0:HALF].bitcast(BF16), ps_p[:, 0:HALF].bitcast(BF16)]
        y_ps = [ps_s, ps_o]

        slots0 = [ps_s, ps_o, ps_x, ps_p]
        USES0 = 13

        def is_step(tt, n):
            return isinstance(tt, int) and tt == n

        QUAD = CT // 2

        def extra(b, tt):
            if not isinstance(tt, int):
                return QUAD
            return QUAD * ((tt > 0) + (tt > TB - 2 and not is_step(b, B - 1)))

        def x_uses(b, tt):
            return b * (TB + CT) + tt + (QUAD + 2 + extra(b, tt))

        def p_uses(b, tt):
            return b * (TB + CT) + tt + (QUAD + extra(b, tt))

        PASSES = ((0, 0), (0, 1), (1, 0))

        block = scope.enter_context(nc.Block())

        def batch(eng, b, step, unroll=False):
            step(b, 0, 0, b * TB)
            if unroll:
                for tt in range(1, 5):
                    step(b, tt, tt % 2, b * TB + tt)
            else:
                with eng.Fori(0, 2) as j:
                    step(b, 2 * j + 1, 1, b * TB + 2 * j + 1)
                    step(b, 2 * j + 2, 0, b * TB + 2 * j + 2)
            for tt in range(5, TB):
                step(b, tt, tt % 2, b * TB + tt)

        @block.sync
        def _(sp):
            sp.dma_start(ctx_f, ctx.rearrange("b k l -> (b k) l").rearrange("(a p) l -> p a l", p=P)).then_inc(got_ctx, 16)
            wkv_rows = Wkv.rearrange("(a p) l -> p a l", p=P)
            wq_rows = Wq.rearrange("(j p) c -> p j c", p=P)
            wout_rows = Wout.rearrange("(a p) c -> p a c", p=P)

            def load_wkv(q):
                sp.dma_start(wkv_f[:, 4 * q:4 * q + 4, :], wkv_rows[:, 4 * q:4 * q + 4, :]).then_inc(got_wkv[q], 16)

            load_wkv(0)
            load_wkv(1)
            for i in range(4):
                quarter = slice(2 * i, 2 * i + 2)
                sp.dma_start(wq_f[:, quarter, :], wq_rows[:, quarter, :]).then_inc(got_wq[i], 16)
            load_wkv(2)
            load_wkv(3)
            for i in range(2):
                half = slice(4 * i, 4 * i + 4)
                sp.dma_start(wout_f[:, half, :], wout_rows[:, half, :]).then_inc(got_wout[i], 16)

            def load_x(to, got, t, e):
                sp.dma_start(to[e], x_rows[bass.ds(t * P, P), :]).then_inc(got[e], 16)

            def load_k(of):
                for to, swap in ((k_hilo, 0), (k_lohi, 1)):
                    for s, rows in enumerate((EVEN, ODD)):
                        for e in range(2):
                            sp.dma_start(to[rows].rearrange("d (j e) k -> d e j k", e=2)[:, e],
                                         of(s ^ swap, e)).then_inc(got_k, 16)

            def load_v(of):
                for s in range(2):
                    for rows in (EVEN, ODD):
                        sp.dma_start(v_diag[rows, s, :, rows], of(s, rows)).then_inc(got_v, 16)

            def move_wq(i):
                pairs = slice(2 * i, 2 * i + 2)
                for src, even_to, odd_to in ((wq_nat_hi[:, pairs, :], EVEN, ODD), (wq_nat_lo[i], ODD, EVEN)):
                    sp.dma_start(wq_heads(0)[even_to, pairs, :], src[EVEN]).then_inc(wq_moved[i], 16)
                    sp.dma_start(wq_heads(1)[odd_to, pairs, :], src[ODD]).then_inc(wq_moved[i], 16)

            for i in range(4):
                sp.wait_ge(wq_split, i + 1)
                move_wq(i)
            sp.wait_ge(k_split, 1)
            load_k(lambda s, e: (k_hi_t, k_lo_t)[s][(EVEN, ODD)[e], :, 0:SK])
            sp.wait_ge(wq_moved[1], 64)
            load_x(xa, got_xa, 0, 0)
            sp.wait_ge(wq_moved[2], 64)
            load_x(xa, got_xa, 1, 1)
            sp.wait_ge(wq_moved[3], 64)
            load_x(xr, got_xr, 0, 0)
            for s, src in enumerate((k_hi_t, k_lo_t)):
                sp.dma_start(kv_dram[s, :, 0:NP, :], src).then_inc(kv_stored, 16)
            for t in range(2, 4):
                sp.wait_ge(xn_ready, t - 1)
                load_x(xa, got_xa, t, t % 2)
            sp.wait_ge(diag_zeroed, 1)
            sp.wait_ge(v_split, 1)
            load_v(lambda s, rows: (v_hi_t, v_lo_t)[s][rows, :, 0:SK])
            for s, src in enumerate((v_hi_t, v_lo_t)):
                sp.dma_start(kv_dram[s, :, NP:NG, :], src).then_inc(kv_stored, 16)
            sp.dma_start(w8_raw[:], Wffn.rearrange("(a p) c -> p a c", p=P)).then_inc(got_w8, 16)

            def next_kv(b):
                sp.wait_ge(p_full, p_uses(b - 1, 0))
                if isinstance(b, int):
                    sp.wait_ge(kv_stored, 64)
                load_k(lambda s, e: kv_dram[s, (EVEN, ODD)[e], 0:NP, bass.ds(b * SK, SK)])
                sp.wait_ge(p_full, p_uses(b - 1, 1))
                load_v(lambda s, rows: kv_dram[s, rows, NP:NG, bass.ds(b * SK, SK)])

            def step(b, tt, e, t):
                known = isinstance(t, int)
                if not known or t + 4 < T:
                    sp.wait_ge(xn_ready, t + 3)
                    load_x(xa, got_xa, t + 4, e)
                if not (known and t == 0):
                    sp.wait_ge(x1_ready, t + 1)
                if not known or t + 1 < T:
                    load_x(xr, got_xr, t + 1, 1 - e)
                if not (known and t == 0):
                    sp.dma_start(x1_dram[bass.ds((t - 1) * P, P), :], x1[1 - e]).then_inc(x1_stored[1 - e], 16)
                if is_step(tt, 0) and not (known and t >= T - TB):
                    next_kv(b + 1)

            batch(sp, 0, step)
            with sp.Fori(1, B - 1) as b:
                batch(sp, b, step)
            batch(sp, B - 1, step, unroll=True)
            sp.wait_ge(x1_ready, T + 1)
            sp.dma_start(x1_dram[(T - 1) * P:T * P, :], x1[(T - 1) % 2]).then_inc(x1_stored[(T - 1) % 2], 16)

            def load_x1(t, i):
                sp.dma_start(x2[i], x1_dram[bass.ds(t * P, P), :]).then_inc(got_x1[i], 16)

            for t in range(4):
                load_x1(t, t)
            for e in range(2):
                sp.wait_ge(x1_stored[e], 16 * (T // 2))
            sp.wait_ge(x1_done, T)
            for t in range(4, X2):
                load_x1(t, t)

            def store_out(t, i):
                sp.wait_ge(sum_ready, t + 1)
                sp.dma_start(out_rows[bass.ds(t * P, P), :], x2[i]).then_inc(out_stored[i], 16)

            with sp.Fori(0, T // X2 - 1) as q:
                for i in range(X2):
                    store_out(q * X2 + i, i)
                    if i % 2:
                        for k in (i - 1, i):
                            sp.wait_ge(out_stored[k], q * 16 + 16)
                            load_x1((q + 1) * X2 + k, k)
            for i in range(X2):
                store_out(T - X2 + i, i)
            for i in range(X2):
                sp.wait_ge(out_stored[i], 16 * (T // X2))
            sp.wait_ge(kv_stored, 64)

        @block.gpsimd
        def _(pool):
            nc.gpsimd.memset(ident[:], 0.0).then_inc(const_made, 1)
            nc.gpsimd.memset(causal[:], 0.0).then_inc(const_made, 1)
            nc.gpsimd.memset(minus_half[:], -0.5).then_inc(const_made, 1)
            pool.wait_ge(const_made, 3)
            nc.gpsimd.affine_select(out=ident[:], in_=ident[:], compare_op=ALU.not_equal, fill=1.0, base=0,
                                    pattern=[[-1, P]], channel_multiplier=1).then_inc(const_made, 1)
            nc.gpsimd.affine_select(out=causal[:], in_=causal[:], compare_op=ALU.is_ge, fill=MASKED, base=0,
                                    pattern=[[-1, SK]], channel_multiplier=1).then_inc(const_made, 1)
            pool.wait_ge(const_made, 5)
            nc.gpsimd.tensor_copy(ident_bf[:], ident[:]).then_inc(const_made, 1)
            nc.gpsimd.memset(flat(v_diag), 0.0).then_inc(diag_zeroed, 1)
            for i in range(2):
                pool.wait_ge(amax_rows, i + 1)
                nc.gpsimd.partition_all_reduce(amax4_all[:, i:i + 1], amax4[:, i:i + 1], P, ROWS_MAX).then_inc(amax_done, 1)

            def inverse_deviation(t, e):
                pool.wait_ge(var_ready, t + 1)
                nc.gpsimd.tensor_tensor(rstd[e][:], veps[e][:], minus_half[:, 0:1], ALU.pow).then_inc(rstd_ready, 1)

            pool.wait_ge(amax_rows, 3)
            nc.gpsimd.partition_all_reduce(amax4_all[:, 2:4], amax4[:, 2:4], P, ROWS_MAX).then_inc(amax_done, 1)
            with pool.Fori(0, TB // 2) as j:
                inverse_deviation(2 * j, 0)
                inverse_deviation(2 * j + 1, 1)
            pool.wait_ge(w_amax_rows, 1)
            nc.gpsimd.partition_all_reduce(small[:, 1:2], small[:, 0:1], P, ROWS_MAX).then_inc(w_amax_done, 1)
            with pool.Fori(TB // 2, T // 2) as j:
                inverse_deviation(2 * j, 0)
                inverse_deviation(2 * j + 1, 1)
            old, new = slice(0, T - TB), slice(T - TB, T)
            pool.wait_ge(var1_ready, 1)
            nc.gpsimd.tensor_tensor(rstd1[:, old], var1[:, old], minus_half[:, old], ALU.pow).then_inc(rstd1_ready, 1)
            pool.wait_ge(var1_ready, 2)
            nc.gpsimd.tensor_tensor(rstd1[:, new], var1[:, new], minus_half[:, new], ALU.pow).then_inc(rstd1_ready, 1)
            pool.wait_ge(x_amax_rows, 1)
            nc.gpsimd.partition_all_reduce(small[:, 3:4], small[:, 2:3], P, ROWS_MAX).then_inc(x_amax_done, 1)

            with pool.Fori(0, T // X2) as q:
                for i in range(X2):
                    pool.wait_ge(y_ready, q * X2 + i + 1)
                    nc.gpsimd.tensor_tensor(x2[i], x2[i], y_t[i % 2], ALU.add).then_inc(sum_ready, 1)

        @block.tensor
        def _(pe):
            use = [0]

            def next_slot():
                n = use[0]
                use[0] += 1
                if n >= 4:
                    pe.wait_ge(turned_read, n - 3)
                return slots0[n % 4]

            pe.wait_ge(const_made, 6)
            pe.wait_ge(got_ctx, 16)
            to = next_slot()
            for lt in range(LT):
                for a in range(KEYS // P):
                    mm = nc.tensor.transpose(to[:, (lt * 4 + a) * P:(lt * 4 + a + 1) * P],
                                             ctx_f[:, a, lt * P:(lt + 1) * P], ident[:])
            mm.then_inc(turned, 1)

            def turn_wkv(q):
                pe.wait_ge(got_wkv[q], 16)
                to = next_slot()
                for lt in range(LT):
                    for a in range(4):
                        mm = nc.tensor.transpose(to[:, (lt * 4 + a) * P:(lt * 4 + a + 1) * P],
                                                 wkv_f[:, 4 * q + a, lt * P:(lt + 1) * P], ident[:])
                mm.then_inc(turned, 1)

            def expand(g2):
                to = next_slot()
                for half in range(2):
                    g = 2 * g2 + half
                    for lt in range(LT):
                        mm = nc.tensor.matmul(to[:, half * HALF:(half + 1) * HALF],
                                              wkv_t[:, lt, g * P:(g + 1) * P], ctx_t[:, lt, :],
                                              start=(lt == 0), stop=(lt == LT - 1))
                mm.then_inc(turned, 1)

            for i in range(2):
                turn_wkv(2 * i)
                turn_wkv(2 * i + 1)
                pe.wait_ge(turned_read, use[0])
                for g2 in range(4 * i, 4 * i + 4):
                    expand(g2)

            def make_m(ct, n):
                to, free, full = ((ps_p, p_free, p_full), (ps_x, x_free, x_full))[ct % 2]
                if not is_step(n, 0):
                    pe.wait_ge(free, n)
                for h in range(NH):
                    cols = to[:, h * SK:(h + 1) * SK]
                    w = wq_stack[:, h, ct * P:(ct + 1) * P]
                    nc.tensor.matmul(cols, w, k_hilo[:, h, :], start=True, stop=False)
                    mm = nc.tensor.matmul(cols, w, k_lohi[:, h, :], start=False, stop=True)
                mm.then_inc(full, 1)

            def make_n(j, n):
                to, free, full = ((ps_x, x_free, x_full), (ps_p, p_free, p_full))[j % 2]
                pe.wait_ge(free, n)
                for i, (vs, ws) in enumerate(PASSES):
                    for half in range(2):
                        cols = slice(half * HALF, (half + 1) * HALF)
                        mm = nc.tensor.matmul(to[:, cols], v_diag[:, vs, j, :], wo_t[:, ws, j, cols],
                                              start=(i == 0), stop=(i == len(PASSES) - 1))
                mm.then_inc(full, 1)

            def split_product(to, left, right, full, weave=lambda c: None):
                for c in range(CT):
                    for i, (ls, rs) in enumerate(PASSES):
                        for half in range(2):
                            cols = slice(half * HALF, (half + 1) * HALF)
                            mm = nc.tensor.matmul(to[:, cols], left[:, ls, c * P:(c + 1) * P], right[:, rs, c, cols],
                                                  start=(c == 0 and i == 0),
                                                  stop=(c == CT - 1 and i == len(PASSES) - 1))
                    if c == CT - 1:
                        mm.then_inc(full, 1)
                    weave(c + 1)

            def turn(to, tile, full, by=ident):
                for c in range(CT):
                    mm = nc.tensor.transpose(to[:, c * P:(c + 1) * P], tile[:, c * P:(c + 1) * P], by[:])
                mm.then_inc(full, 1)

            def turn_w8(a):
                pe.wait_ge(w8_ready, a + 1)
                turn(w8_ps[a], w8_q[a % 2], w8_full, ident_bf)

            def step(b, tt, e, t):
                known = isinstance(t, int)
                last = known and t >= T - TB
                xb, pb = x_uses(b, tt), p_uses(b, tt)
                if last and tt >= 2:
                    pe.wait_ge(w8_read, tt - 1)
                pe.wait_ge(p_ready, t + 1)
                pe.wait_ge(p_free, pb)
                turn(ps_p, pr, p_full)
                n_here = is_step(tt, 0)
                if n_here:
                    pe.wait_ge(got_v, 64 * b + 64)
                if not known or t + 1 < T:
                    m_last = is_step(tt, TB - 1)
                    pe.wait_ge(x_free, xb - m_last)
                    pe.wait_ge(s_read, t + 1)

                    def between(c):
                        if n_here and c < CT:
                            make_n(c, (xb, pb + 1)[c % 2] + c // 2)
                        if m_last and c == CT - 1:
                            pe.wait_ge(x_free, xb)

                    between(0)
                    split_product(ps_s, xt_buf, m_buf, s_full, between)
                if not known or t + 2 < T:
                    pe.wait_ge(xn_ready, t + 3)
                    if n_here:
                        pe.wait_ge(x_free, xb + QUAD)
                    turn(ps_x, xn[e], x_full)
                if known and t == T - 1:
                    pe.wait_ge(s_read, T)
                    turn_w8(tt - 1)
                pe.wait_ge(p_free, pb + 1 + QUAD * n_here)
                if last and 1 <= tt < TB - 1:
                    turn_w8(tt - 1)
                pe.wait_ge(x1_ready, t + 1)
                if is_step(tt, TB - 2) and not last:
                    pe.wait_ge(got_k, 128 * b + 256)

                    def next_m(c):
                        make_m(c - 1, (pb + 1, xb + 1)[(c - 1) % 2] + (c - 1) // 2)

                    split_product(ps_o, pt_buf, n_buf, o_full, next_m)
                else:
                    split_product(ps_o, pt_buf, n_buf, o_full)

            def turn_wout(j):
                if j >= 2:
                    pe.wait_ge(wt_free, j - 1)
                to = (ps_s, ps_o)[j % 2]
                for a in range(CT):
                    mm = nc.tensor.transpose(to[:, a * P:(a + 1) * P], wout_f[:, a, j * P:(j + 1) * P], ident[:])
                mm.then_inc(wt_full, 1)

            pe.wait_ge(turned_read, USES0)
            for i in range(2):
                pe.wait_ge(got_wout[i], 16)
            turn_wout(0)
            pe.wait_ge(got_k, 128)
            for i in range(4):
                pe.wait_ge(wq_moved[i], 64)
            for c in range(CT):
                make_m(c, c // 2)
                if c == 1:
                    pe.wait_ge(wout_sum, CT)
                if c >= 1:
                    turn_wout(c)
            pe.wait_ge(x_free, QUAD)
            pe.wait_ge(xn_ready, 1)
            turn(ps_x, xn[0], x_full)
            pe.wait_ge(wt_free, NP - 1)
            pe.wait_ge(p_free, QUAD)
            pe.wait_ge(x_free, QUAD + 1)
            split_product(ps_s, xt_buf, m_buf, s_full)
            pe.wait_ge(xn_ready, 2)
            turn(ps_x, xn[1], x_full)

            with pe.Fori(0, B - 1) as b:
                batch(pe, b, step)
            batch(pe, B - 1, step, unroll=True)
            pe.wait_ge(w8_read, CT - 1)
            turn_w8(CT - 1)

            def turn_r(t, e, first):
                pe.wait_ge(r_ready, t + 1)
                if not first:
                    pe.wait_ge(rt_ready, t - 1)
                turn(r_ps[e], r_t[e], r_full, ident_bf)

            def linear(t, e, first, between=lambda: None):
                pe.wait_ge(rt_ready, t + 1)
                if not first:
                    pe.wait_ge(y_ready, t - 1)
                for c in range(CT):
                    for half in range(2):
                        cols = slice(half * HALF, (half + 1) * HALF)
                        mm = nc.tensor.matmul(y_ps[e][:, cols], rt_t[e][:, c * P:(c + 1) * P], w8_t[:, c, cols],
                                              start=(c == 0), stop=(c == CT - 1))
                    if c == CT // 2:
                        between()
                mm.then_inc(y_full, 1)

            pe.wait_ge(w8_read, CT)
            pe.wait_ge(x1_ready, T + 1)
            turn_r(0, 0, True)
            linear(0, 0, True, lambda: turn_r(1, 1, True))
            turn_r(2, 0, False)
            linear(1, 1, True)
            with pe.Fori(1, T // 2 - 1) as j:
                turn_r(2 * j + 1, 1, False)
                linear(2 * j, 0, False)
                turn_r(2 * j + 2, 0, False)
                linear(2 * j + 1, 1, False)
            turn_r(T - 1, 1, False)
            linear(T - 2, 0, False)
            linear(T - 1, 1, False)

        @block.scalar
        def _(act):
            def copy_out(n, to):
                act.wait_ge(turned, n + 1)
                nc.scalar.activation(to, slots0[n % 4][:].rearrange("p (a k) -> p a k", a=2),
                                     ACT.Copy).then_inc(turned_read, 1)

            def split_wq_hi(i):
                pairs = slice(2 * i, 2 * i + 2)
                nc.scalar.activation(wq_nat_hi[:, pairs, :], wq_f[:, pairs, :], ACT.Copy,
                                     scale=to_f16[:, 0:1]).then_inc(wq_hi, 1)

            def copy_wkv(n, q):
                copy_out(n, wkv_t[:, :, q * HALF:(q + 1) * HALF])

            def copy_kv(n, to, g2):
                copy_out(n, to[:, 2 * g2:2 * g2 + 2, :])

            copy_out(0, ctx_t)
            copy_wkv(1, 0)
            copy_wkv(2, 1)
            for g2 in range(4):
                if g2 == 3:
                    act.wait_ge(scales_made, 1)
                    split_wq_hi(0)
                copy_kv(3 + g2, k_f, g2)
            copy_wkv(7, 2)
            copy_wkv(8, 3)
            for i in range(1, 4):
                split_wq_hi(i)
            act.wait_ge(scales_made, 2)
            for i in range(2):
                part = slice(4 * i, 4 * i + 4)
                nc.scalar.activation(k_hi_t[:, part, :], k_f[:, part, :], ACT.Copy, scale=to_f16[:, 1:2]).then_inc(k_hi, 1)
            for g2 in range(4):
                copy_kv(9 + g2, v_f, g2)
            act.wait_ge(turned_read, USES0)
            for a in range(CT):
                if a % 4 == 0:
                    act.wait_ge(got_wout[a // 4], 16)
                if a > 0:
                    act.wait_ge(wout_sum, a)
                nc.scalar.activation(ps_o[:], wout_f[:, a, :], ACT.Abs,
                                     accum_out=wout_sums[:, a:a + 1]).then_inc(wout_sum, 1)

            def take_hi(to, slot, full, n, scale, done):
                act.wait_ge(full, n)
                nc.scalar.activation(to, slot[:], ACT.Copy, scale=scale).then_inc(done, 1)

            def take_n(c, n):
                slot, full, done = ((ps_x, x_full, x_hi), (ps_p, p_full, p_hi))[c % 2]
                take_hi(n_buf[:, 0, c, :], slot, full, n + 1, N_SCALE, done)

            def take_m(c, n):
                slot, full, done = ((ps_p, p_full, p_hi), (ps_x, x_full, x_hi))[c % 2]
                take_hi(m_buf[:, 0, c, :], slot, full, n + 1, M_SCALE, done)

            def exponentials(t):
                act.wait_ge(s_read, t + 1)
                nc.scalar.activation(ex, sub, ACT.Exp, scale=score_scale[:]).then_inc(exp_done, 1)

            def deviations(t, e):
                act.wait_ge(mean_ready, t + 1)
                nc.scalar.activation(dev, x1[e], ACT.Abs, bias=neg_mean[e][:]).then_inc(dev_ready, 1)

            def quotients(a):
                if a == 0:
                    act.wait_ge(w_scale_made, 1)
                else:
                    act.wait_ge(w8_ready, a)
                nc.scalar.activation(w_tmp[0], w8_raw[:, a, :], ACT.Copy, scale=small[:, 5:6]).then_inc(w_quot, 1)

            def copy_w8(a):
                act.wait_ge(w8_full, a + 1)
                nc.scalar.activation(w8_t[:, :, a * P:(a + 1) * P], w8_ps[a].rearrange("p (c o) -> p c o", c=CT),
                                     ACT.Copy).then_inc(w8_read, 1)

            def step(b, tt, e, t):
                known = isinstance(t, int)
                last = known and t >= T - TB
                xb, pb = x_uses(b, tt), p_uses(b, tt)
                take_hi(pt_buf[:, 0, :], ps_p, p_full, pb + 1, P_SCALE, p_hi)
                grown = 0
                grow_n = lambda c: take_n(c, (xb, pb + 1)[c % 2] + c // 2)
                if is_step(tt, 0):
                    grown = QUAD
                    if known and t == 0:
                        act.wait_ge(kv_stored, 64)
                    for c in range(3):
                        grow_n(c)
                if not (known and t == 0):
                    deviations(t - 1, 1 - e)
                if last:
                    quotients(tt)
                if is_step(tt, 0):
                    for c in range(3, CT):
                        grow_n(c)
                if not known or t + 2 < T:
                    take_hi(xt_buf[:, 0, :], ps_x, x_full, xb + grown + 1, XN_SCALE, x_hi)
                if last and tt >= 1:
                    copy_w8(tt - 1)
                if not known or t + 1 < T:
                    exponentials(t + 1)
                if is_step(tt, TB - 2) and not last:
                    for c in range(CT):
                        take_m(c, (pb + 1, xb + 1)[c % 2] + c // 2)

            def take_wout(j):
                act.wait_ge(wt_full, j + 1)
                nc.scalar.activation(wo_t[:, 0, j, :], (ps_s, ps_o)[j % 2][:], ACT.Copy,
                                     scale=to_f16[:, 2:3]).then_inc(wt_hi, 1)

            act.wait_ge(scales_made, 3)
            for c in range(CT):
                take_m(c, c // 2)
                if c % 2 == 0:
                    act.wait_ge(wq_moved[c // 2], 64)
                take_wout(c)
            act.wait_ge(kv_stored, 32)
            take_hi(xt_buf[:, 0, :], ps_x, x_full, QUAD + 1, XN_SCALE, x_hi)
            nc.scalar.activation(v_hi_t, v_f, ACT.Copy, scale=to_f16[:, 3:4]).then_inc(v_hi, 1)
            take_hi(xt_buf[:, 0, :], ps_x, x_full, QUAD + 2, XN_SCALE, x_hi)
            exponentials(0)
            batch(act, 0, step)
            with act.Fori(1, B - 1) as b:
                batch(act, b, step)
            batch(act, B - 1, step, unroll=True)
            copy_w8(CT - 1)
            deviations(T - 1, 1)

            def values(t, i, e, first):
                act.wait_ge(got_x1[i], (t - i) * (16 // X2) + 16)
                if not first:
                    act.wait_ge(g_done, t - 1)
                nc.scalar.activation(u_t[e], x2[i], ACT.Identity, bias=quant_b20[:, bass.ds(t, 1)],
                                     scale=quant_a20[:, bass.ds(t, 1)]).then_inc(u_ready, 1)
                if e == 0 and not is_step(t, 0):
                    if not first:
                        act.wait_ge(a_done, t - 1)
                    nc.scalar.activation(v_t[e], x2[i], ACT.Identity, bias=quant_b[:, bass.ds(t, 1)],
                                         scale=quant_a[:, bass.ds(t, 1)]).then_inc(v_ready, 1)

            def copy_rt(t, e, first):
                act.wait_ge(r_full, t + 1)
                if not first:
                    act.wait_ge(y_full, t - 1)
                nc.scalar.activation(rt_t[e], r_ps[e], ACT.Copy).then_inc(rt_ready, 1)

            def scaled(t, e, first):
                act.wait_ge(y_full, t + 1)
                if not first:
                    act.wait_ge(sum_ready, t - 1)
                nc.scalar.activation(y_t[e], y_ps[e][:], ACT.Copy, scale=small[:, 8:9]).then_inc(y_ready, 1)

            act.wait_ge(quant_ready, 1)
            for t in range(3):
                values(t, t, t % 2, t < 2)
            for t in range(2):
                copy_rt(t, t, True)
                values(t + 3, t + 3, (t + 3) % 2, False)

            def step2(t, i, first=False):
                e, ahead = i % 2, (i + 5) % X2
                scaled(t, e, first)
                copy_rt(t + 2, e, False)
                values(t + 5, ahead, ahead % 2, False)

            for t in range(3):
                step2(t, t, t < 2)
            with act.Fori(0, T // X2 - 1) as q:
                for i in range(3, 3 + X2):
                    step2(q * X2 + i, i % X2)
            for t in range(T - 5, T):
                scaled(t, t % 2, False)
                if t + 2 < T:
                    copy_rt(t + 2, t % 2, False)

        @block.vector
        def _(dve):
            steps = [0]

            def then(ins):
                steps[0] += 1
                ins.then_inc(dve_step, 1)
                dve.wait_ge(dve_step, steps[0])

            def powers(cols, n):
                dve.wait_ge(amax_done, n)
                then(nc.vector.tensor_scalar(amax4_all[:, cols], amax4_all[:, cols], AMAX_FLOOR, None, ALU.max))
                then(nc.vector.tensor_scalar(amax4_all[:, cols].bitcast(U32), amax4_all[:, cols].bitcast(U32),
                                             EXPONENT_BITS, None, ALU.bitwise_and))
                then(nc.vector.tensor_scalar(from_f16[:, cols], amax4_all[:, cols], 1.0 / AMAX_TO, None, ALU.mult))
                nc.vector.reciprocal(to_f16[:, cols], from_f16[:, cols]).then_inc(scales_made, 1)
                dve.wait_ge(scales_made, n)

            for i in range(4):
                dve.wait_ge(got_wq[i], 16)
                nc.vector.tensor_reduce(small[:, 4 + i:5 + i], wq_f[:, 2 * i:2 * i + 2, :], AX.XY, ALU.max,
                                        apply_absolute_value=True).then_inc(dve_step, 1)
            steps[0] = 4
            dve.wait_ge(dve_step, steps[0])
            nc.vector.tensor_reduce(amax4[:, 0:1], small[:, 4:8], AX.X, ALU.max).then_inc(amax_rows, 1)
            powers(slice(0, 1), 1)

            def split_wq_lo(i):
                pairs = slice(2 * i, 2 * i + 2)
                dve.wait_ge(wq_hi, i + 1)
                nc.vector.scalar_tensor_tensor(out=wq_nat_lo[i], in0=wq_f[:, pairs, :], scalar=to_f16[:, 0:1],
                                               in1=wq_nat_hi[:, pairs, :], op0=ALU.mult,
                                               op1=ALU.subtract).then_inc(wq_split, 1)

            split_wq_lo(0)
            dve.wait_ge(turned_read, 7)
            nc.vector.tensor_reduce(amax4[:, 1:2], k_f, AX.XY, ALU.max, apply_absolute_value=True).then_inc(amax_rows, 1)
            split_wq_lo(1)
            powers(slice(1, 2), 2)
            then(nc.vector.tensor_scalar(score_scale[:], from_f16[:, 0:1], from_f16[:, 1:2],
                                         1.0 / (M_SCALE * XN_SCALE * HD ** 0.5), ALU.mult, ALU.mult))
            split_wq_lo(2)
            split_wq_lo(3)
            for i in range(2):
                part = slice(4 * i, 4 * i + 4)
                dve.wait_ge(k_hi, i + 1)
                lo = nc.vector.scalar_tensor_tensor(out=k_lo_t[:, part, :], in0=k_f[:, part, :], scalar=to_f16[:, 1:2],
                                                    in1=k_hi_t[:, part, :], op0=ALU.mult, op1=ALU.subtract)
                lo.then_inc((dve_step, k_split)[i], 1)
            steps[0] += 1
            dve.wait_ge(turned_read, USES0)
            then(nc.vector.tensor_reduce(amax4[:, 3:4], v_f, AX.XY, ALU.max, apply_absolute_value=True))

            def take_lo(to, hi, slot, n, scale, hi_done, free):
                dve.wait_ge(hi_done, n)
                nc.vector.scalar_tensor_tensor(out=to, in0=slot[:], scalar=scale, in1=hi, op0=ALU.mult,
                                               op1=ALU.subtract).then_inc(free, 1)

            def take_n(c, n):
                slot, done, free = ((ps_x, x_hi, x_free), (ps_p, p_hi, p_free))[c % 2]
                take_lo(n_buf[:, 1, c, :], n_buf[:, 0, c, :], slot, n + 1, N_SCALE, done, free)

            def take_m(c, n):
                slot, done, free = ((ps_p, p_hi, p_free), (ps_x, x_hi, x_free))[c % 2]
                take_lo(m_buf[:, 1, c, :], m_buf[:, 0, c, :], slot, n + 1, M_SCALE, done, free)

            def variance(t, e):
                dve.wait_ge(got_xa[e], (t - e) * 8 + 16)
                for half in range(2):
                    nc.vector.bn_stats(stats_a[:, half, :], xa[e][:, half * HALF:(half + 1) * HALF]).then_inc(a_stats, 1)
                dve.wait_ge(a_stats, 2 * t + 2)
                nc.vector.memset(wait_carrier[:], 0.0)
                nc.vector.bn_aggr(mv_a[e][:], stats_a[:].rearrange("p a b -> p (a b)")).then_inc(a_aggr, 1)
                dve.wait_ge(a_aggr, t + 1)
                nc.vector.tensor_scalar(veps[e][:], mv_a[e][:, 1:2], LN_EPS, None, ALU.add).then_inc(var_ready, 1)

            def normalise(t, e):
                dve.wait_ge(rstd_ready, t + 1)
                nc.vector.tensor_scalar(xn[e], xa[e], mv_a[e][:, 0:1], rstd[e][:], ALU.subtract,
                                        ALU.mult).then_inc(xn_ready, 1)

            def heads(ap):
                return ap.rearrange("p (h k) -> p h k", h=NH)

            def across(ap):
                return ap.unsqueeze(2).to_broadcast([P, NH, SK])

            def mask_scores(t):
                dve.wait_ge(s_full, t + 1)
                nc.vector.tensor_tensor(heads(ps_s[:]), heads(ps_s[:]),
                                        causal[:].unsqueeze(1).to_broadcast([P, NH, SK]), ALU.add).then_inc(masked, 1)

            def maxima(t, masks=None):
                if masks is None:
                    dve.wait_ge(s_full, t + 1)
                else:
                    dve.wait_ge(masked, masks)
                nc.vector.tensor_reduce(hmax[:], heads(ps_s[:]), AX.X, ALU.max).then_inc(max_done, 1)
                dve.wait_ge(max_done, t + 1)
                nc.vector.tensor_tensor(heads(sub), heads(ps_s[:]), across(hmax[:]), ALU.subtract).then_inc(s_read, 1)

            def sums(t):
                dve.wait_ge(exp_done, t + 1)
                nc.vector.tensor_reduce(hsum[:], heads(ex), AX.X, ALU.add).then_inc(sum_done, 1)

            def probabilities(t):
                dve.wait_ge(sum_done, t + 1)
                nc.vector.reciprocal(hinv[:], hsum[:]).then_inc(inv_done, 1)
                dve.wait_ge(inv_done, t + 1)
                nc.vector.tensor_tensor(heads(pr), heads(ex), across(hinv[:]), ALU.mult).then_inc(p_ready, 1)

            def residual(t, e, stored=True):
                dve.wait_ge(o_full, t + 1)
                dve.wait_ge(got_xr[e], (t - e) * 8 + 16)
                if stored:
                    dve.wait_ge(x1_stored[e], (t - e) * 8)
                nc.vector.scalar_tensor_tensor(out=x1[e], in0=ps_o[:], scalar=out_scale[:], in1=xr[e], op0=ALU.mult,
                                               op1=ALU.add).then_inc(x1_ready, 1)

            def statistics(t, e):
                dve.wait_ge(x1_ready, t + 2)
                for half in range(2):
                    nc.vector.bn_stats(stats_b[:, half, :], x1[e][:, half * HALF:(half + 1) * HALF]).then_inc(b_stats, 1)
                dve.wait_ge(b_stats, 2 * t + 2)
                nc.vector.memset(wait_carrier[:], 0.0)
                nc.vector.bn_aggr(mv_b[:], stats_b[:].rearrange("p a b -> p (a b)")).then_inc(b_aggr, 1)
                dve.wait_ge(b_aggr, t + 1)
                nc.vector.tensor_scalar(neg_mean[e][:], mv_b[:, 0:1], -1.0, None, ALU.mult).then_inc(mean_ready, 1)
                nc.vector.tensor_copy(mean1[:, bass.ds(t, 1)], mv_b[:, 0:1]).then_inc(kept, 1)
                nc.vector.tensor_scalar(var1[:, bass.ds(t, 1)], mv_b[:, 1:2], LN_EPS, None, ALU.add).then_inc(kept, 1)

            def peak(t):
                dve.wait_ge(dev_ready, t + 1)
                nc.vector.tensor_reduce(peak1[:, bass.ds(t, 1)], dev, AX.X, ALU.max).then_inc(x1_done, 1)

            def round_e4m3(rounded, v, u, g, s):
                then(nc.vector.tensor_scalar(g.bitcast(U32), u.bitcast(U32), EXPONENT_BITS, HALF_BIT,
                                             ALU.bitwise_and, ALU.bitwise_or))
                then(nc.vector.scalar_tensor_tensor(out=s, in0=g, scalar=ROUND_LEAST, in1=v, op0=ALU.max, op1=ALU.add))
                return nc.vector.scalar_tensor_tensor(out=rounded, in0=g, scalar=ROUND_LEAST, in1=s, op0=ALU.max,
                                                      op1=ALU.subtract)

            def quantise_w8(a):
                SPLIT16 = 2.0 ** 8 + 1.0
                w, s, v, u = w_tmp
                dve.wait_ge(w_quot, a + 1)
                then(nc.vector.scalar_tensor_tensor(out=s, in0=w, scalar=SPLIT16, in1=w, op0=ALU.mult, op1=ALU.subtract))
                then(nc.vector.scalar_tensor_tensor(out=v, in0=w, scalar=SPLIT16, in1=s, op0=ALU.mult, op1=ALU.subtract))
                then(nc.vector.tensor_scalar(u, v, ROUND_SHIFT, None, ALU.mult))
                if a >= 2:
                    dve.wait_ge(w8_full, a - 1)
                round_e4m3(w8_q[a % 2], v, u, w, s).then_inc(w8_ready, 1)
                dve.wait_ge(w8_ready, a + 1)

            def step(b, tt, e, t):
                known = isinstance(t, int)
                last = known and t >= T - TB
                xb, pb = x_uses(b, tt), p_uses(b, tt)
                if known and t == T - 1:
                    residual(t - 1, 1 - e)
                take_lo(pt_buf[:, 1, :], pt_buf[:, 0, :], ps_p, pb + 1, P_SCALE, p_hi, p_free)
                norm = not known or t + 3 < T
                grown = 0
                grow_n = lambda c: take_n(c, (xb, pb + 1)[c % 2] + c // 2)
                grow_m = lambda c: take_m(c, (pb + 1, xb + 1)[c % 2] + c // 2)
                if is_step(tt, 0):
                    grown = QUAD
                    grow_n(0)
                if not (known and t in (0, T - 1)):
                    residual(t - 1, 1 - e, stored=not (known and t < 3))
                if is_step(tt, 0):
                    grow_n(1)
                if not (known and t == 0):
                    statistics(t - 1, 1 - e)
                if is_step(tt, 0):
                    grow_n(2)
                if norm:
                    variance(t + 3, 1 - e)
                if is_step(tt, 0):
                    grow_n(3)
                if not (known and t == 0):
                    peak(t - 1)
                if norm:
                    normalise(t + 3, 1 - e)
                if is_step(tt, 0):
                    for c in range(4, CT):
                        grow_n(c)
                if last and tt == TB - 2:
                    quantise_w8(tt)
                if not known or t + 1 < T:
                    if is_step(tt, TB - 1):
                        mask_scores(t + 1)
                        maxima(t + 1, masks=b + 2)
                    else:
                        maxima(t + 1)
                if not known or t + 2 < T:
                    take_lo(xt_buf[:, 1, :], xt_buf[:, 0, :], ps_x, xb + grown + 1, XN_SCALE, x_hi, x_free)
                grow = is_step(tt, TB - 2) and not last
                if not known or t + 1 < T:
                    sums(t + 1)
                if grow:
                    grow_m(0)
                if not known or t + 1 < T:
                    probabilities(t + 1)
                if grow:
                    for c in range(1, CT):
                        grow_m(c)
                if known and t == 3:
                    dve.wait_ge(got_w8, 16)
                    nc.vector.tensor_reduce(small[:, 0:1], w8_raw[:], AX.XY, ALU.max,
                                            apply_absolute_value=True).then_inc(w_amax_rows, 1)
                if known and t == 6:
                    dve.wait_ge(w_amax_done, 1)
                    then(nc.vector.tensor_scalar(small[:, 4:5], small[:, 1:2], 1.0 / E4M3_MAX, 1e-12, ALU.mult, ALU.max))
                    nc.vector.reciprocal(small[:, 5:6], small[:, 4:5]).then_inc(w_scale_made, 1)
                if last:
                    if tt == 1:
                        dve.wait_ge(kept, 2 * (T - TB))
                        nc.vector.tensor_copy(small[:, 15:16], mv_b[:, 0:1]).then_inc(var1_ready, 1)
                    if tt != TB - 2:
                        quantise_w8(tt)

            def take_wout(j):
                dve.wait_ge(wt_hi, j + 1)
                nc.vector.scalar_tensor_tensor(out=wo_t[:, 1, j, :], in0=(ps_s, ps_o)[j % 2][:], scalar=to_f16[:, 2:3],
                                               in1=wo_t[:, 0, j, :], op0=ALU.mult, op1=ALU.subtract).then_inc(wt_free, 1)

            dve.wait_ge(wout_sum, CT)
            nc.vector.tensor_reduce(amax4[:, 2:3], wout_sums[:], AX.X, ALU.add).then_inc(amax_rows, 1)
            powers(slice(2, 4), 3)
            then(nc.vector.tensor_scalar(out_scale[:], from_f16[:, 2:3], from_f16[:, 3:4],
                                         1.0 / (N_SCALE * P_SCALE), ALU.mult, ALU.mult))
            for c in range(CT):
                take_m(c, c // 2)
                take_wout(c)
                if c == 2:
                    variance(0, 0)
                if c == 3:
                    normalise(0, 0)
            take_lo(xt_buf[:, 1, :], xt_buf[:, 0, :], ps_x, QUAD + 1, XN_SCALE, x_hi, x_free)
            variance(1, 1)
            normalise(1, 1)
            dve.wait_ge(v_hi, 1)
            nc.vector.scalar_tensor_tensor(out=v_lo_t, in0=v_f, scalar=to_f16[:, 3:4], in1=v_hi_t, op0=ALU.mult,
                                           op1=ALU.subtract).then_inc(v_split, 1)
            variance(2, 0)
            mask_scores(0)
            maxima(0, masks=1)
            take_lo(xt_buf[:, 1, :], xt_buf[:, 0, :], ps_x, QUAD + 2, XN_SCALE, x_hi, x_free)
            normalise(2, 0)
            sums(0)
            probabilities(0)
            nc.vector.memset(wait_carrier[:], 0.0).then_inc(x1_ready, 1)
            batch(dve, 0, step, unroll=True)
            with dve.Fori(1, B - 1) as b:
                batch(dve, b, step)
            batch(dve, B - 1, step, unroll=True)
            residual(T - 1, 1)
            statistics(T - 1, 1)
            dve.wait_ge(kept, 2 * T)
            nc.vector.tensor_copy(small[:, 15:16], mv_b[:, 0:1]).then_inc(var1_ready, 1)
            peak(T - 1)

            dve.wait_ge(rstd1_ready, 2)
            dve.wait_ge(x1_done, T)
            then(nc.vector.tensor_tensor(quant_a20, peak1[:], rstd1[:], ALU.mult))
            nc.vector.tensor_reduce(small[:, 2:3], quant_a20, AX.X, ALU.max).then_inc(x_amax_rows, 1)
            dve.wait_ge(x_amax_done, 1)
            then(nc.vector.tensor_scalar(small[:, 6:7], small[:, 3:4], 1.0 / E4M3_MAX, 1e-12, ALU.mult, ALU.max))
            then(nc.vector.reciprocal(small[:, 7:8], small[:, 6:7]))
            then(nc.vector.tensor_scalar(quant_a[:], rstd1[:], small[:, 7:8], None, ALU.mult))
            then(nc.vector.scalar_tensor_tensor(out=quant_b[:], in0=mean1[:], scalar=-1.0, in1=quant_a[:], op0=ALU.mult,
                                                op1=ALU.mult))
            nc.vector.tensor_scalar(small[:, 8:9], small[:, 6:7], small[:, 4:5], None, ALU.mult).then_inc(dve_step, 1)
            nc.vector.tensor_scalar(quant_a20, quant_a[:], ROUND_SHIFT, None, ALU.mult).then_inc(dve_step, 1)
            steps[0] += 2
            dve.wait_ge(dve_step, steps[0])
            nc.vector.tensor_scalar(quant_b20, quant_b[:], ROUND_SHIFT, None, ALU.mult).then_inc(quant_ready, 1)

            def constant_g(t, e, first=False):
                dve.wait_ge(u_ready, t + 1)
                if not first:
                    dve.wait_ge(r_ready, t - 1)
                nc.vector.tensor_scalar(g_t[e].bitcast(U32), u_t[e].bitcast(U32), EXPONENT_BITS, HALF_BIT,
                                        ALU.bitwise_and, ALU.bitwise_or).then_inc(g_done, 1)

            def value_v(t, i, first=False):
                dve.wait_ge(got_x1[i], (t - i) * (16 // X2) + 16)
                if not first:
                    dve.wait_ge(a_done, t - 1)
                nc.vector.tensor_scalar(v_t[1], x2[i], quant_a[:, bass.ds(t, 1)], quant_b[:, bass.ds(t, 1)], ALU.mult,
                                        ALU.add).then_inc(v_odd, 1)

            def rounded(t, e, first=False):
                dve.wait_ge(a_done, t + 1)
                if not first:
                    dve.wait_ge(r_full, t - 1)
                nc.vector.scalar_tensor_tensor(out=r_t[e], in0=g_t[e], scalar=ROUND_LEAST, in1=a_t[e], op0=ALU.max,
                                               op1=ALU.subtract).then_inc(r_ready, 1)

            def two_tiles(base, i, before, last=False):
                t, pairs = base + i, before + i // 2 + 1
                first = isinstance(t, int) and t == 0
                dve.wait_ge(g_done, t + 1)
                dve.wait_ge(v_ready, pairs)
                nc.vector.scalar_tensor_tensor(out=a_t[0], in0=g_t[0], scalar=ROUND_LEAST, in1=v_t[0], op0=ALU.max,
                                               op1=ALU.add).then_inc(a_done, 1)
                if first:
                    rounded(t, 0, first)
                value_v(t + 1, i + 1, first)
                constant_g(t + 1, 1, first)
                if not first:
                    rounded(t, 0, first)
                dve.wait_ge(g_done, t + 2)
                dve.wait_ge(v_odd, pairs)
                nc.vector.scalar_tensor_tensor(out=a_t[1], in0=g_t[1], scalar=ROUND_LEAST, in1=v_t[1], op0=ALU.max,
                                               op1=ALU.add).then_inc(a_done, 1)
                if not last:
                    constant_g(t + 2, 0)
                rounded(t + 1, 1, first)

            dve.wait_ge(got_x1[0], 16)
            nc.vector.tensor_scalar(v_t[0], x2[0], quant_a[:, 0:1], quant_b[:, 0:1], ALU.mult, ALU.add).then_inc(v_ready, 1)
            constant_g(0, 0, True)
            for i in range(0, X2, 2):
                two_tiles(0, i, 0)
            with dve.Fori(1, T // X2 - 1) as q:
                for i in range(0, X2, 2):
                    two_tiles(q * X2, i, q * (X2 // 2))
            for i in range(0, X2, 2):
                two_tiles(T - X2, i, (T - X2) // 2, last=(i == X2 - 2))


_INS = ['x', 'ctx_512', 'L0_xattn_Wq', 'L0_xattn_Wkv_expand', 'L0_xattn_Wout', 'L0_ffn_weight']
_OUTS = [((8, 1024, 1024), 'float32')]


def kernel(**inputs):
    import numpy as _np
    import concourse.bacc as _bacc
    from concourse import mybir as _mybir
    from concourse.bass_utils import run_bass_kernel_spmd as _run

    nc = _bacc.Bacc("TRN2", target_bir_lowering=False, num_devices=1)
    arrays, args = {}, []
    for name in _INS:
        a = _np.ascontiguousarray(inputs[name])
        arrays[f"in_{name}_dram"] = a
        args.append(nc.dram_tensor(f"in_{name}_dram", a.shape, _mybir.dt.from_np(a.dtype), kind="ExternalInput").ap())
    for i, (shape, dtype) in enumerate(_OUTS):
        dt = _mybir.dt.from_np(_np.dtype(dtype))
        args.append(nc.dram_tensor(f"out_{i}_dram", shape, dt, kind="ExternalOutput").ap())
    xattn_ffn_kernel(nc, *args)
    r = _run(nc, [arrays], core_ids=[0])
    return r.results[0]["out_0_dram"]
```
